# Optimizing a Trainium2 kernel written in Bass

```python
import numpy as np
import jax
import jax.numpy as jnp

def _softmax(x, axis=-1):
    return jax.nn.softmax(x, axis=axis)

def _gelu(x):
    return jax.nn.gelu(x, approximate=True)

def _silu(x):
    return jax.nn.silu(x)

def _sigmoid(x):
    return jax.nn.sigmoid(x)

def _layernorm(x, axis=-1, eps=1e-05):
    m = jnp.mean(x, axis=axis, keepdims=True)
    v = jnp.var(x, axis=axis, keepdims=True)
    return (x - m) / jnp.sqrt(v + eps)

def _scatter_add(tgt, idx, src, axis=0):
    return tgt.at[idx].add(src)

def _segment_sum(src, seg, n):
    return jax.ops.segment_sum(src, seg, n)
kernel_name = 'mk_sandwich_d1_jaxref_r8_4e39e8'

def setup_inputs(seed: int=0):
    np.random.seed(seed)
    _w = jnp.asarray

    def _L0_attn_setup():
        import jax, jax.numpy as jnp
        import numpy as np
        B, T, D = (2, 256, 256)
        H = 8
        KEY_DIM, VAL_DIM = (128, 256)
        HK, HV = (KEY_DIM // H, VAL_DIM // H)
        LOW_RANK = 16
        GATE_NORM = 16.0
        CHUNK = 64
        HIDDEN = (D * 4 * 2 // 3 + 63) // 64 * 64
        EPS = 1e-06

        def rmsnorm(x, w):
            return x * jax.lax.rsqrt(jnp.mean(x * x, axis=-1, keepdims=True) + EPS) * w

        def _gla(h, wq, wk, wv, gk_w1, gk_w2, gk_b, wg, gnorm_w, wo):
            Bb, Tt, _ = h.shape
            nc = Tt // CHUNK

            def split(t, hd):
                t = t.reshape(Bb, nc, CHUNK, H, hd)
                return jnp.transpose(t, (1, 0, 3, 2, 4))
            q = split(h @ wq, HK) * HK ** (-0.5)
            k = split(h @ wk, HK)
            v = split(h @ wv, HV)
            g = split(jax.nn.log_sigmoid(h @ gk_w1 @ gk_w2 + gk_b) / GATE_NORM, HK)
            mask = jnp.tril(jnp.ones((CHUNK, CHUNK), jnp.float32))

            def step(S, inp):
                qc, kc, vc, gc = inp
                b = jnp.cumsum(gc, axis=-2)
                qe = qc * jnp.exp(b)
                A = jnp.einsum('bhik,bhjk->bhij', qe, kc * jnp.exp(-b)) * mask
                o = jnp.einsum('bhck,bhkv->bhcv', qe, S) + jnp.einsum('bhij,bhjv->bhiv', A, vc)
                bl = b[:, :, -1:, :]
                S = jnp.exp(bl[:, :, 0, :])[..., None] * S + jnp.einsum('bhck,bhcv->bhkv', kc * jnp.exp(bl - b), vc)
                return (S, o)
            S0 = jnp.zeros((Bb, H, HK, HV), h.dtype)
            _, o = jax.lax.scan(step, S0, (q, k, v, g))
            o = jnp.transpose(o, (1, 0, 3, 2, 4)).reshape(Bb, Tt, H, HV)
            gate = (h @ wg).reshape(Bb, Tt, H, HV)
            o = rmsnorm(o, gnorm_w) * gate * jax.nn.sigmoid(gate)
            return o.reshape(Bb, Tt, VAL_DIM) @ wo
        key = jax.random.key(seed)
        ks = jax.random.split(key, 12)
        w = lambda k, s: jax.random.normal(k, s, jnp.float32) * 0.02
        return {'x': jax.random.normal(ks[0], (B, T, D), jnp.float32), 'norm1_w': jnp.ones((D,), jnp.float32), 'wq': w(ks[1], (D, KEY_DIM)), 'wk': w(ks[2], (D, KEY_DIM)), 'wv': w(ks[3], (D, VAL_DIM)), 'gk_w1': w(ks[4], (D, LOW_RANK)), 'gk_w2': w(ks[5], (LOW_RANK, KEY_DIM)), 'gk_b': jnp.zeros((KEY_DIM,), jnp.float32), 'wg': w(ks[6], (D, VAL_DIM)), 'gnorm_w': jnp.ones((HV,), jnp.float32), 'wo': w(ks[7], (VAL_DIM, D)), 'ffn_norm_w': jnp.ones((D,), jnp.float32), 'w_gate': w(ks[8], (D, HIDDEN)), 'w_up': w(ks[9], (D, HIDDEN)), 'w_down': w(ks[10], (HIDDEN, D))}
    _L0_attn_in = _L0_attn_setup()

    def _L0_ffn_setup():
        import jax, jax.numpy as jnp
        import numpy as np
        H = 256
        NH = 16
        NOPE = 128
        ROPE = 64
        VD = 128
        QHD = NOPE + ROPE
        E = 16
        I = 176
        TOPK = 4
        NSH = 2
        SHI = I * NSH
        EPS = 1e-06
        B, S = (2, 128)

        def rmsnorm(x, w):
            return x * jax.lax.rsqrt(jnp.mean(x * x, axis=-1, keepdims=True) + EPS) * w
        key = jax.random.key(seed)
        ks = jax.random.split(key, 12)
        sd = lambda fan_in: 1.0 / np.sqrt(fan_in)
        return {'hidden_states': jax.random.normal(ks[0], (B, S, H), jnp.float32), 'positions': jnp.broadcast_to(jnp.arange(S, dtype=jnp.int32), (B, S)), 'ln1_w': jnp.ones((H,), jnp.float32), 'ln2_w': jnp.ones((H,), jnp.float32), 'q_w': jax.random.normal(ks[1], (NH * QHD, H), jnp.float32) * sd(H), 'kv_w': jax.random.normal(ks[2], (NH * (NOPE + VD) + ROPE, H), jnp.float32) * sd(H), 'o_w': jax.random.normal(ks[3], (H, NH * VD), jnp.float32) * sd(NH * VD), 'gate_w': jax.random.normal(ks[4], (E, H), jnp.float32) * sd(H), 'w1': jax.random.normal(ks[5], (E, 2 * I, H), jnp.float32) * sd(H), 'w2': jax.random.normal(ks[6], (E, H, I), jnp.float32) * sd(I), 'sh_gu_w': jax.random.normal(ks[7], (2 * SHI, H), jnp.float32) * sd(H), 'sh_down_w': jax.random.normal(ks[8], (H, SHI), jnp.float32) * sd(SHI)}
    _L0_ffn_in = _L0_ffn_setup()
    _d = {'L0_attn_x': _L0_attn_in['x'], 'L0_attn_norm1_w': _L0_attn_in['norm1_w'], 'L0_attn_wq': _L0_attn_in['wq'], 'L0_attn_wk': _L0_attn_in['wk'], 'L0_attn_wv': _L0_attn_in['wv'], 'L0_attn_gk_w1': _L0_attn_in['gk_w1'], 'L0_attn_gk_w2': _L0_attn_in['gk_w2'], 'L0_attn_gk_b': _L0_attn_in['gk_b'], 'L0_attn_wg': _L0_attn_in['wg'], 'L0_attn_gnorm_w': _L0_attn_in['gnorm_w'], 'L0_attn_wo': _L0_attn_in['wo'], 'L0_attn_ffn_norm_w': _L0_attn_in['ffn_norm_w'], 'L0_attn_w_gate': _L0_attn_in['w_gate'], 'L0_attn_w_up': _L0_attn_in['w_up'], 'L0_attn_w_down': _L0_attn_in['w_down'], 'L0_ffn_positions': _L0_ffn_in['positions'], 'L0_ffn_ln1_w': _L0_ffn_in['ln1_w'], 'L0_ffn_ln2_w': _L0_ffn_in['ln2_w'], 'L0_ffn_q_w': _L0_ffn_in['q_w'], 'L0_ffn_kv_w': _L0_ffn_in['kv_w'], 'L0_ffn_o_w': _L0_ffn_in['o_w'], 'L0_ffn_gate_w': _L0_ffn_in['gate_w'], 'L0_ffn_w1': _L0_ffn_in['w1'], 'L0_ffn_w2': _L0_ffn_in['w2'], 'L0_ffn_sh_gu_w': _L0_ffn_in['sh_gu_w'], 'L0_ffn_sh_down_w': _L0_ffn_in['sh_down_w']}
    _x0 = _d['L0_attn_x']
    _d['L0_attn_x'] = jax.random.normal(jax.random.fold_in(jax.random.key(seed), 1), (2, 1024, 256), dtype=_x0.dtype)
    del _x0
    return _d

def reference(L0_attn_x, L0_attn_norm1_w, L0_attn_wq, L0_attn_wk, L0_attn_wv, L0_attn_gk_w1, L0_attn_gk_w2, L0_attn_gk_b, L0_attn_wg, L0_attn_gnorm_w, L0_attn_wo, L0_attn_ffn_norm_w, L0_attn_w_gate, L0_attn_w_up, L0_attn_w_down, L0_ffn_positions, L0_ffn_ln1_w, L0_ffn_ln2_w, L0_ffn_q_w, L0_ffn_kv_w, L0_ffn_o_w, L0_ffn_gate_w, L0_ffn_w1, L0_ffn_w2, L0_ffn_sh_gu_w, L0_ffn_sh_down_w):

    def _L0_attn_ref(x, norm1_w, wq, wk, wv, gk_w1, gk_w2, gk_b, wg, gnorm_w, wo, ffn_norm_w, w_gate, w_up, w_down):
        import jax, jax.numpy as jnp
        import numpy as np
        B, T, D = (2, 256, 256)
        H = 8
        KEY_DIM, VAL_DIM = (128, 256)
        HK, HV = (KEY_DIM // H, VAL_DIM // H)
        LOW_RANK = 16
        GATE_NORM = 16.0
        CHUNK = 64
        HIDDEN = (D * 4 * 2 // 3 + 63) // 64 * 64
        EPS = 1e-06

        def rmsnorm(x, w):
            return x * jax.lax.rsqrt(jnp.mean(x * x, axis=-1, keepdims=True) + EPS) * w

        def _gla(h, wq, wk, wv, gk_w1, gk_w2, gk_b, wg, gnorm_w, wo):
            Bb, Tt, _ = h.shape
            nc = Tt // CHUNK

            def split(t, hd):
                t = t.reshape(Bb, nc, CHUNK, H, hd)
                return jnp.transpose(t, (1, 0, 3, 2, 4))
            q = split(h @ wq, HK) * HK ** (-0.5)
            k = split(h @ wk, HK)
            v = split(h @ wv, HV)
            g = split(jax.nn.log_sigmoid(h @ gk_w1 @ gk_w2 + gk_b) / GATE_NORM, HK)
            mask = jnp.tril(jnp.ones((CHUNK, CHUNK), jnp.float32))

            def step(S, inp):
                qc, kc, vc, gc = inp
                b = jnp.cumsum(gc, axis=-2)
                qe = qc * jnp.exp(b)
                A = jnp.einsum('bhik,bhjk->bhij', qe, kc * jnp.exp(-b)) * mask
                o = jnp.einsum('bhck,bhkv->bhcv', qe, S) + jnp.einsum('bhij,bhjv->bhiv', A, vc)
                bl = b[:, :, -1:, :]
                S = jnp.exp(bl[:, :, 0, :])[..., None] * S + jnp.einsum('bhck,bhcv->bhkv', kc * jnp.exp(bl - b), vc)
                return (S, o)
            S0 = jnp.zeros((Bb, H, HK, HV), h.dtype)
            _, o = jax.lax.scan(step, S0, (q, k, v, g))
            o = jnp.transpose(o, (1, 0, 3, 2, 4)).reshape(Bb, Tt, H, HV)
            gate = (h @ wg).reshape(Bb, Tt, H, HV)
            o = rmsnorm(o, gnorm_w) * gate * jax.nn.sigmoid(gate)
            return o.reshape(Bb, Tt, VAL_DIM) @ wo
        h = rmsnorm(x, norm1_w)
        x = x + _gla(h, wq, wk, wv, gk_w1, gk_w2, gk_b, wg, gnorm_w, wo)
        h2 = rmsnorm(x, ffn_norm_w)
        ffn = jax.nn.silu(h2 @ w_gate) * (h2 @ w_up) @ w_down
        return x + ffn

    def _L0_ffn_ref(hidden_states, positions, ln1_w, ln2_w, q_w, kv_w, o_w, gate_w, w1, w2, sh_gu_w, sh_down_w):
        import jax, jax.numpy as jnp
        import numpy as np
        H = 256
        NH = 16
        NOPE = 128
        ROPE = 64
        VD = 128
        QHD = NOPE + ROPE
        E = 16
        I = 176
        TOPK = 4
        NSH = 2
        SHI = I * NSH
        EPS = 1e-06
        B, S = (2, 128)

        def rmsnorm(x, w):
            return x * jax.lax.rsqrt(jnp.mean(x * x, axis=-1, keepdims=True) + EPS) * w
        b, s, h = hidden_states.shape
        x = rmsnorm(hidden_states, ln1_w)
        q = jnp.einsum('bsh,dh->bsd', x, q_w).reshape(b, s, NH, QHD)[..., :NOPE]
        kv = jnp.einsum('bsh,dh->bsd', x, kv_w)
        k = kv[..., :NH * NOPE].reshape(b, s, NH, NOPE)
        v = kv[..., NH * NOPE:NH * (NOPE + VD)].reshape(b, s, NH, VD)
        scale = QHD ** (-0.5)
        scores = jnp.einsum('bqnd,bknd->bnqk', q, k) * scale
        causal = jnp.tril(jnp.ones((s, s), bool))
        scores = jnp.where(causal, scores, -1000000000.0)
        p = jax.nn.softmax(scores, axis=-1)
        attn = jnp.einsum('bnqk,bknd->bqnd', p, v).reshape(b, s, NH * VD)
        attn_out = jnp.einsum('bsd,hd->bsh', attn, o_w)
        hid = hidden_states + attn_out
        x2 = rmsnorm(hid, ln2_w).reshape(-1, h)
        logits = x2 @ gate_w.T
        probs = jax.nn.softmax(logits, axis=-1)
        top_w, top_i = jax.lax.top_k(probs, TOPK)
        top_w = top_w / jnp.sum(top_w, axis=-1, keepdims=True)
        wfull = jnp.sum(jax.nn.one_hot(top_i, E, dtype=x2.dtype) * top_w[..., None], axis=1)
        gu = jnp.einsum('th,eih->tei', x2, w1)
        g, u = (gu[..., :I], gu[..., I:])
        act = jax.nn.silu(g) * u
        down = jnp.einsum('tei,ehi->teh', act, w2)
        routed = jnp.einsum('te,teh->th', wfull, down)
        sgu = x2 @ sh_gu_w.T
        sg, su = (sgu[..., :SHI], sgu[..., SHI:])
        shared = jax.nn.silu(sg) * su @ sh_down_w.T
        return hid + (routed + shared).reshape(b, s, h)
    x = L0_attn_x
    x = x + _layernorm(_L0_attn_ref(_layernorm(x, axis=-1), L0_attn_norm1_w, L0_attn_wq, L0_attn_wk, L0_attn_wv, L0_attn_gk_w1, L0_attn_gk_w2, L0_attn_gk_b, L0_attn_wg, L0_attn_gnorm_w, L0_attn_wo, L0_attn_ffn_norm_w, L0_attn_w_gate, L0_attn_w_up, L0_attn_w_down), axis=-1)
    x = x + _layernorm(_L0_ffn_ref(_layernorm(x, axis=-1), L0_ffn_positions, L0_ffn_ln1_w, L0_ffn_ln2_w, L0_ffn_q_w, L0_ffn_kv_w, L0_ffn_o_w, L0_ffn_gate_w, L0_ffn_w1, L0_ffn_w2, L0_ffn_sh_gu_w, L0_ffn_sh_down_w), axis=-1)
    return x

_drawn_inputs = setup_inputs


def setup_inputs(seed=0):
    import zlib

    import numpy as np

    out = dict(_drawn_inputs(seed))
    spreads = {'L0_attn_norm1_w': (1.0, 0.6),
     'L0_attn_gk_b': (0.0, 0.8),
     'L0_attn_gnorm_w': (1.0, 0.6),
     'L0_attn_ffn_norm_w': (1.0, 0.6),
     'L0_ffn_ln1_w': (1.0, 0.6),
     'L0_ffn_ln2_w': (1.0, 0.2)}
    factors = {'L0_attn_gk_w1': 8.0,
     'L0_attn_gk_w2': 8.0,
     'L0_attn_w_gate': 3.344,
     'L0_attn_w_up': 3.3,
     'L0_attn_w_down': 3.276}
    for name, (base, spread) in spreads.items():
        noise = np.random.default_rng([zlib.crc32(name.encode()), seed]).standard_normal(out[name].shape)
        drawn = base * np.exp(spread * noise) if base else spread * noise
        out[name] = jnp.asarray(drawn.astype(out[name].dtype))
    for name, factor in factors.items():
        out[name] = (out[name] * factor).astype(out[name].dtype)
    return out
```

```python
from contextlib import ExitStack

import concourse.bass as bass
from concourse import mybir

F32 = mybir.dt.float32
F32R = mybir.dt.float32r
ALU = mybir.AluOpType
ACT = mybir.ActivationFunctionType
AX_X = mybir.AxisListType.X

P = 128
D = 256
DC = D // P
NB = 4
BT = 512
HID = 6 * P
NCH = 8
EPS_LN = 1e-5
EPS_RMS = 1e-6
MASKED = -3e10
PAIRS = 9
HEADS = 16
QHD = 192


class Steps:

    def __init__(self, names):
        self.index = {n: k for k, n in enumerate(names)}
        self.names = list(names)
        self.per = len(self.names)
        self.made = 0
        assert len(self.index) == self.per

    def at(self, name, i):
        return (i + 1) * self.per + (self.index[name] + 1)

    def latest(self, i, needs):
        return i * self.per + max((d + 1) * self.per + self.index[n] + 1 for n, d in needs)

    def one(self, name):
        assert self.names[self.made % self.per] == name, (name, self.names[self.made % self.per])
        self.made += 1
        return 1


def product3(nc, out, w, x, first, last):
    nc.tensor.matmul(out, w[0], x[0], start=first, stop=False)
    nc.tensor.matmul(out, w[0], x[1], start=False, stop=False)
    return nc.tensor.matmul(out, w[1], x[0], start=False, stop=last)


def gla_layer(nc, ctx, sb, sem, psum, keep, dram):
    st = ExitStack()
    with st:
        def tb(name, shape, dt=F32):
            return st.enter_context(nc.sbuf_tensor(name, shape, dt))

        def ps_sem(name):
            return sem("gla_" + name)

        WC = 2 * 768 + 2 * D + 2 * 1536 + 6 * D
        O_QKVG, O_WO, O_GU, O_WD = 0, 1536, 1536 + 512, 1536 + 512 + 3072
        w_hi, w_lo = tb("gw_hi", [P, WC], F32R), tb("gw_lo", [P, WC], F32R)
        w_in = tb("gw_in", [P, WC])
        w_low = tb("gw_low", [P, DC, 16])
        w_up = tb("gw_up", [16, P])
        cols = tb("gcols", [P, 8])
        ones = tb("gones", [P, P])
        hblk = tb("ghblk", [P, P])
        tri = tb("gtri", [P, 64])
        hmask = tb("ghmask", [P, 8])
        bmask = tb("gbmask", [P, 8, 32])
        notfirst = tb("gnotfirst", [P, BT])
        ident = keep["ident"]

        x = tb("g_x", [P, DC, BT])
        xcsq = tb("g_xcsq", [P, 2, DC, BT])
        xc, sq = xcsq[:, 0], xcsq[:, 1]
        rs = tb("g_rs", [P, DC, BT])
        xn = tb("g_xn", [P, DC, BT])
        h = tb("g_h", [P, DC, BT])
        hhi, hlo = tb("g_hhi", [P, DC, BT], F32R), tb("g_hlo", [P, DC, BT], F32R)
        sg = tb("g_sg", [P, DC, BT])
        v = tb("g_v", [P, 4, D])
        lb, cum = tb("g_lb", [P, BT]), tb("g_cum", [P, BT])
        qe, ke = tb("g_qe", [P, BT]), tb("g_ke", [P, BT])
        eb = tb("g_eb", [P, BT])
        kdT = tb("g_kdT", [P, 4, P])
        a_hi = [tb(f"g_ahi{k}", [P, BT], F32R) for k in range(2)]
        a_lo = [tb(f"g_alo{k}", [P, BT], F32R) for k in range(2)]
        af = [tb(f"g_af{k}", [P, BT]) for k in range(2)]
        low, la = af[0][0:16, :], af[1]
        qbd = w_in[:, 0:NCH * 512].rearrange("p (c h i) -> p c h i", c=NCH, h=8)
        atm = w_in[:, 4096:4096 + 2048].rearrange("p (a h i) -> p a h i", a=4, h=8)
        dsm = xcsq.rearrange("p a c n -> p (a c n)").rearrange("p (a b n) -> p a b n", a=4, b=2)
        S = tb("g_S", [P, 2, 5, D])

        s_w, s_x, s_x1 = ps_sem("weights_loaded"), [ps_sem("x_loaded")], ps_sem("x1_stored")
        s_const = ps_sem("constants")
        CONSTS = 25
        s_whi, s_wlo = ps_sem("weights_hi"), ps_sem("weights_lo")
        pe_s, act_s, dve_s = ps_sem("tensor_steps"), ps_sem("scalar_steps"), ps_sem("vector_steps")

        def norm_names(n, rms):
            return ([n + "_mean", n + "_var"], [n + "_sq", n + "_lnv", n + "_rstd"] +
                    ([n + "_lnr", n + "_rrms", n + "_hi"] if rms else []),
                    [n + "_xc", n + "_xn"] + ([n + "_v1", n + "_v2", n + "_h0", n + "_h1", n + "_lo"] if rms else []))

        nA, nB, nC = norm_names("in", True), norm_names("out", False), norm_names("next", True)
        PE = Steps(nA[0] + ["q", "k", "low", "gate", "v", "z", "kdT"] + ["dS"] +
                   [f"A{p}" for p in range(4)] + ["o", "osum", "wo", "rms2"] +
                   [x_ for j in range(6) for x_ in ([f"gu{j}"] + ([f"down{j - 1}"] if j else []))] + ["down5"] +
                   nB[0] + nC[0])
        AC = Steps(nA[1] + ["silu", "low", "v", "abs", "e", "ln", "eb", "enb", "edk", "kdT",
                            "osq0", "osq1", "lno", "ro", "oghi", "sq2", "ln2", "r2", "h2hi"] +
                   [x_ for j in range(6) for x_ in (f"silu{j}", f"acthi{j}")] + nB[1] + nC[1])
        DV = Steps(nA[2] + ["zmin", "graw", "cum", "dcum", "qe", "ke", "kd"] + [f"qbd{c}" for c in range(8)] +
                   [f"dsm{c}" for c in range(4)] + [f"S{c}" for c in range(8)] + [f"atm{p}" for p in range(4)] +
                   ["og0", "og1", "og", "oglo", "xa", "h20", "h21", "h2lo"] +
                   [x_ for j in range(6) for x_ in (f"act{j}", f"actlo{j}")] + ["xb", "carry"] +
                   nB[2] + ["x1"] + nC[2])

        def bank(k, n=1):
            return psum[:, k:k + n, :] if n > 1 else psum[:, k, :]

        def whl(off, n):
            return w_hi[:, off:off + n], w_lo[:, off:off + n]

        def bc2(ap):
            return ap.unsqueeze(1).broadcast_to([P, DC, BT])

        def o_view(half):
            return psum[:, half:half + 6:5, 0:256].rearrange("p r (a t) -> p r a t", a=4)

        def o_sums():
            return psum[:, 2:8:5, :]

        block = st.enter_context(nc.Block())

        @block.sync
        def _(sp):
            sp.wait_ge(s_const, 1)
            qkvg = w_in[:, 0:1536].rearrange("p (c n) -> p c n", c=2)
            at = 0
            for name, n in (("wq", 128), ("wk", 128), ("wv", 256), ("wg", 256)):
                sp.dma_start(qkvg[:, :, at:at + n], dram[name].rearrange("(c p) n -> p c n", p=P)).then_inc(s_w, 16)
                at += n
            sp.dma_start(w_in[:, O_WO:O_GU].rearrange("p (c n) -> p c n", c=2),
                         dram["wo"].rearrange("(c p) n -> p c n", p=P)).then_inc(s_w, 16)
            gu = w_in[:, O_GU:O_WD].rearrange("p (c g n) -> p c g n", c=2, g=2)
            for g, name in enumerate(("w_gate", "w_up")):
                sp.dma_start(gu[:, :, g, 0:704], dram[name].rearrange("(c p) n -> p c n", p=P)).then_inc(s_w, 16)
            wd = w_in[:, O_WD:WC].rearrange("p (c n) -> p c n", c=6)
            sp.dma_start(wd[:, 0:5, :], dram["w_down"][0:640, :].rearrange("(c p) n -> p c n", p=P)).then_inc(s_w, 16)
            sp.dma_start(wd[0:64, 5, :], dram["w_down"][640:704, :]).then_inc(s_w, 16)
            sp.dma_start(w_low[:], dram["gk_w1"].rearrange("(c p) n -> p c n", p=P)).then_inc(s_w, 16)
            sp.dma_start(w_up[:], dram["gk_w2"]).then_inc(s_w, 16)
            sp.dma_start(cols[:], dram["cols"]).then_inc(s_w, 16)
            with sp.Fori(0, NB) as i:
                sp.wait_ge(dve_s, DV.at("x1", i - 1))
                sp.dma_start(x[:], dram["xT"][:, :, bass.ds(i * BT, BT)]).then_inc(s_x[0], 16)
                sp.wait_ge(dve_s, DV.at("x1", i))
                sp.dma_start(dram["x1"][:, :, bass.ds(i * BT, BT)], h[:]).then_inc(s_x1, 16)
            sp.wait_ge(s_x1, 16 * NB)

        @block.gpsimd
        def _(pool):
            step = [0]

            def made(ins):
                step[0] += 1
                ins.then_inc(s_const, 1)
                pool.wait_ge(s_const, step[0])

            made(nc.gpsimd.memset(w_in[:], 0.0))
            made(nc.gpsimd.memset(ones[:], 1.0 / D))
            made(nc.gpsimd.memset(hblk[:], 0.0))
            for g in range(4):
                made(nc.gpsimd.memset(hblk[32 * g:32 * g + 32, 32 * g:32 * g + 32], 1.0 / 32))
            made(nc.gpsimd.memset(tri[:], 1.0))
            for r in range(2):
                t = tri[64 * r:64 * r + 64, :]
                made(nc.gpsimd.affine_select(out=t, in_=t, compare_op=ALU.is_ge, fill=0.0, base=0,
                                             pattern=[[1, 64]], channel_multiplier=-1))
            made(nc.gpsimd.memset(hmask[:], 1.0))
            made(nc.gpsimd.affine_select(out=hmask[:], in_=hmask[:], compare_op=ALU.is_ge, fill=0.0, base=0,
                                         pattern=[[-16, 8]], channel_multiplier=1))
            made(nc.gpsimd.affine_select(out=hmask[:], in_=hmask[:], compare_op=ALU.is_ge, fill=0.0, base=15,
                                         pattern=[[16, 8]], channel_multiplier=-1))
            made(nc.gpsimd.memset(bmask[:], 1.0))
            made(nc.gpsimd.affine_select(out=bmask[:], in_=bmask[:], compare_op=ALU.is_ge, fill=0.0, base=0,
                                         pattern=[[-16, 8], [0, 32]], channel_multiplier=1))
            made(nc.gpsimd.affine_select(out=bmask[:], in_=bmask[:], compare_op=ALU.is_ge, fill=0.0, base=15,
                                         pattern=[[16, 8], [0, 32]], channel_multiplier=-1))
            made(nc.gpsimd.memset(notfirst[:], 1.0))
            made(nc.gpsimd.memset(notfirst[:].rearrange("p (c t) -> p c t", c=8)[:, :, 0:1], 0.0))
            made(nc.gpsimd.memset(S[:], 0.0))
            made(nc.gpsimd.memset(keep["eps"][:, 0:1], EPS_LN))
            made(nc.gpsimd.memset(keep["eps"][:, 1:2], EPS_RMS))
            made(nc.gpsimd.memset(ident[:], 0.0))
            made(nc.gpsimd.affine_select(out=ident[:], in_=ident[:], compare_op=ALU.not_equal, fill=1.0, base=0,
                                         pattern=[[-1, P]], channel_multiplier=1))
            made(nc.gpsimd.memset(keep["cmask"][:], 0.0))
            made(nc.gpsimd.affine_select(out=keep["cmask"][:], in_=keep["cmask"][:], compare_op=ALU.is_ge,
                                         fill=MASKED, base=0, pattern=[[-1, P]], channel_multiplier=1))
            assert step[0] == CONSTS

        @block.tensor
        def _(pe):
            def stat(name, src, k, wait_sem, value):
                pe.wait_ge(wait_sem, value)
                nc.tensor.matmul(bank(k), ones[:], src[:, 0, :], start=True, stop=False)
                return nc.tensor.matmul(bank(k), ones[:], src[:, 1, :], start=False, stop=True).then_inc(pe_s, PE.one(name))

            pe.wait_ge(s_const, CONSTS)
            pe.wait_ge(s_whi, 1)
            pe.wait_ge(s_wlo, 1)
            pe.sem_inc(pe_s, PE.per)
            with pe.Fori(0, NB) as i:
                pe.wait_ge(dve_s, DV.at("next_lo", i - 1))
                pe.wait_ge(act_s, AC.at("next_hi", i - 1))
                stat("in_mean", x, 7, s_x[0], (i + 1) * 16)
                stat("in_var", sq, 6, act_s, AC.at("in_sq", i))
                pe.wait_ge(dve_s, DV.at("in_lo", i))
                pe.wait_ge(act_s, AC.at("in_hi", i))

                def proj(k, off):
                    for c in range(DC):
                        last = product3(nc, bank(k), whl(c * 768 + off, P), (hhi[:, c, :], hlo[:, c, :]), c == 0, c == 1)
                    return last

                proj(0, 0).then_inc(pe_s, PE.one("q"))
                proj(1, 128).then_inc(pe_s, PE.one("k"))
                for c in range(DC):
                    last = nc.tensor.matmul(psum[0:16, 2, :], w_low[:, c, :], h[:, c, :], start=c == 0, stop=c == 1)
                last.then_inc(pe_s, PE.one("low"))
                proj(3, 512)
                proj(4, 640).then_inc(pe_s, PE.one("gate"))
                for t in range(4):
                    for c in range(DC):
                        last = product3(nc, psum[:, 5 + t // 2, (t % 2) * D:(t % 2) * D + D],
                                        (hhi[:, c, t * P:(t + 1) * P], hlo[:, c, t * P:(t + 1) * P]),
                                        whl(c * 768 + 256, D), c == 0, c == 1)
                last.then_inc(pe_s, PE.one("v"))
                pe.wait_ge(act_s, AC.at("low", i))
                nc.tensor.matmul(bank(7), w_up[:], low, start=True, stop=True).then_inc(pe_s, PE.one("z"))
                pe.wait_ge(dve_s, DV.at("kd", i))
                for t in range(4):
                    last = nc.tensor.transpose(psum[:, 2, t * P:(t + 1) * P], lb[:, t * P:(t + 1) * P], ident[:])
                last.then_inc(pe_s, PE.one("kdT"))
                pe.wait_ge(act_s, AC.at("kdT", i))
                for r in range(2):
                    for p in range(4):
                        last = nc.tensor.matmul(psum[:, (0, 5)[r] + p // 2, (p % 2) * D:(p % 2) * D + D],
                                                kdT[64 * r:64 * r + 64, p, :], v[64 * r:64 * r + 64, p, :],
                                                start=True, stop=True)
                last.then_inc(pe_s, PE.one("dS"))
                for p in range(4):
                    pe.wait_ge(dve_s, DV.at(f"qbd{2 * p + 1}" if p < 2 else f"atm{p - 2}", i))
                    if p == 0:
                        pe.wait_ge(act_s, AC.at("silu", i))
                    for r in range(2):
                        c = 2 * p + r
                        last = nc.tensor.matmul(psum[64 * r:64 * r + 64, 3 + p % 2, :], ke[:, c * 64:c * 64 + 64],
                                                qbd[:, c], start=True, stop=True)
                    last.then_inc(pe_s, PE.one(f"A{p}"))
                pe.wait_ge(dve_s, DV.at("atm3", i))
                for c in range(8):
                    p, r, b, t = c // 2, c % 2, c // 4, c % 4
                    for half in range(2):
                        k = (0, 5)[r] + half
                        nc.tensor.matmul(psum[:, k, p * 64:p * 64 + 64], S[:, b, t, half * P:half * P + P],
                                         qe[:, c * 64:c * 64 + 64], start=True, stop=False, skip_group_check=True)
                        for g in range(4):
                            hd = 4 * half + g
                            last = nc.tensor.matmul(psum[32 * g:32 * g + 32, k, p * 64:p * 64 + 64],
                                                    v[64 * r:64 * r + 64, p, hd * 32:hd * 32 + 32],
                                                    atm[64 * r:64 * r + 64, p, hd, :], start=False, stop=True,
                                                    skip_group_check=True)
                last.then_inc(pe_s, PE.one("o"))
                pe.wait_ge(act_s, AC.at("osq1", i))
                for half in range(2):
                    last = nc.tensor.matmul(bank((2, 7)[half]), hblk[:], sq[:, half, :], start=True, stop=True)
                last.then_inc(pe_s, PE.one("osum"))
                pe.wait_ge(act_s, AC.at("oghi", i))
                pe.wait_ge(dve_s, DV.at("oglo", i))
                for m in range(2):
                    for c in range(DC):
                        last = product3(nc, bank(3 + m), whl(O_WO + c * D + m * P, P), (hhi[:, c, :], hlo[:, c, :]),
                                        c == 0, c == 1)
                last.then_inc(pe_s, PE.one("wo"))
                stat("rms2", sq, 7, act_s, AC.at("sq2", i))
                pe.wait_ge(act_s, AC.at("h2hi", i))
                pe.wait_ge(dve_s, DV.at("h2lo", i))

                def down(j):
                    pe.wait_ge(act_s, AC.at(f"acthi{j}", i))
                    pe.wait_ge(dve_s, DV.at(f"actlo{j}", i))
                    for m in range(2):
                        last = product3(nc, bank(3 + m), whl(O_WD + j * D + m * P, P),
                                        (a_hi[j % 2][:], a_lo[j % 2][:]), j == 0, j == 5)
                    last.then_inc(pe_s, PE.one(f"down{j}"))

                for j in range(6):
                    if j >= 2:
                        pe.wait_ge(dve_s, DV.at(f"act{j - 2}", i))
                    for g in range(2):
                        for c in range(DC):
                            last = product3(nc, bank((0, 1, 5, 6)[2 * (j % 2) + g]),
                                            whl(O_GU + c * 1536 + g * 768 + j * P, P), (hhi[:, c, :], hlo[:, c, :]),
                                            c == 0, c == 1)
                    last.then_inc(pe_s, PE.one(f"gu{j}"))
                    if j:
                        down(j - 1)
                down(5)
                stat("out_mean", xn, 7, dve_s, DV.at("xb", i))
                stat("out_var", sq, 6, act_s, AC.at("out_sq", i))
                stat("next_mean", h, 7, dve_s, DV.at("x1", i))
                stat("next_var", sq, 6, act_s, AC.at("next_sq", i))

        @block.scalar
        def _(act):
            def do(name, out, in_, func, **kw):
                return nc.scalar.activation(out, in_, func, **kw).then_inc(act_s, AC.one(name))

            def stats(n, i, rms):
                act.wait_ge(dve_s, DV.at(n + "_xc", i))
                do(n + "_sq", sq, xc, ACT.Square)
                act.wait_ge(pe_s, PE.at(n + "_var", i))
                do(n + "_lnv", rs[:, 0, :], bank(6), ACT.Ln, bias=keep["eps"][:, 0:1])
                act.wait_ge(act_s, AC.at(n + "_lnv", i))
                do(n + "_rstd", rs[:, 0, :], rs[:, 0, :], ACT.Exp, scale=-0.5)
                if rms:
                    act.wait_ge(dve_s, DV.at(n + "_v2", i))
                    do(n + "_lnr", rs[:, 1, :], rs[:, 1, :], ACT.Ln, bias=keep["eps"][:, 1:2])
                    act.wait_ge(act_s, AC.at(n + "_lnr", i))
                    do(n + "_rrms", rs[:, 1, :], rs[:, 1, :], ACT.Exp, scale=-0.5)

            act.wait_ge(s_const, CONSTS)
            act.wait_ge(s_w, 16 * 12)
            nc.scalar.activation(w_hi[:], w_in[:], ACT.Copy).then_inc(s_whi, 1)
            act.sem_inc(act_s, AC.per)
            with act.Fori(0, NB) as i:
                stats("in", i, True)
                act.wait_ge(dve_s, DV.at("in_h1", i))
                do("in_hi", hhi[:], h[:], ACT.Copy)
                act.wait_ge(pe_s, PE.at("gate", i))
                do("silu", sg[:], bank(3, 2), ACT.Silu)
                act.wait_ge(pe_s, PE.at("low", i))
                do("low", low, psum[0:16, 2, :], ACT.Copy)
                act.wait_ge(pe_s, PE.at("v", i))
                do("v", v[:].rearrange("p (a t) n -> p a (t n)", a=2), bank(5, 2), ACT.Copy)
                act.wait_ge(pe_s, PE.at("z", i))
                do("abs", la[:], bank(7), ACT.Abs, bias=cols[:, 6:7])
                act.wait_ge(act_s, AC.at("abs", i))
                do("e", la[:], la[:], ACT.Exp, scale=-1.0)
                act.wait_ge(act_s, AC.at("e", i))
                do("ln", la[:], la[:], ACT.Ln, bias=1.0)
                act.wait_ge(dve_s, DV.at("cum", i))
                do("eb", eb[:], cum[:], ACT.Exp, scale=1.0 / 16)
                do("enb", ke[:], cum[:], ACT.Exp, scale=-1.0 / 16)
                act.wait_ge(dve_s, DV.at("dcum", i))
                do("edk", lb[:], lb[:], ACT.Exp, scale=1.0 / 16)
                act.wait_ge(pe_s, PE.at("kdT", i))
                do("kdT", kdT[:].rearrange("p t n -> p (t n)"), bank(2), ACT.Copy)
                act.wait_ge(pe_s, PE.at("o", i))
                for half in range(2):
                    do(f"osq{half}", sq[:, half, :].rearrange("p (a r t) -> p r a t", a=4, r=2), o_view(half), ACT.Square)
                act.wait_ge(pe_s, PE.at("osum", i))
                do("lno", rs[:], o_sums(), ACT.Ln, bias=keep["eps"][:, 1:2])
                act.wait_ge(act_s, AC.at("lno", i))
                do("ro", rs[:], rs[:], ACT.Exp, scale=-0.5)
                act.wait_ge(dve_s, DV.at("og", i))
                do("oghi", hhi[:], h[:], ACT.Copy)
                act.wait_ge(dve_s, DV.at("xa", i))
                do("sq2", sq, xn[:], ACT.Square)
                act.wait_ge(pe_s, PE.at("rms2", i))
                do("ln2", rs[:, 1, :], bank(7), ACT.Ln, bias=keep["eps"][:, 1:2])
                act.wait_ge(act_s, AC.at("ln2", i))
                do("r2", rs[:, 1, :], rs[:, 1, :], ACT.Exp, scale=-0.5)
                act.wait_ge(dve_s, DV.at("h21", i))
                do("h2hi", hhi[:], h[:], ACT.Copy)
                for j in range(6):
                    act.wait_ge(pe_s, PE.at(f"gu{j}", i))
                    do(f"silu{j}", sg[:, j % 2, :], bank((0, 5)[j % 2]), ACT.Silu)
                    act.wait_ge(dve_s, DV.at(f"act{j}", i))
                    if j >= 2:
                        act.wait_ge(pe_s, PE.at(f"down{j - 2}", i))
                    do(f"acthi{j}", a_hi[j % 2][:], af[j % 2][:], ACT.Copy)
                stats("out", i, False)
                stats("next", i, True)
                act.wait_ge(dve_s, DV.at("next_h1", i))
                do("next_hi", keep["xx_hi"][:, :, bass.ds(i * BT, BT)], sq, ACT.Copy)

        @block.vector
        def _(dve):
            def tt(name, out, a, b, op):
                return nc.vector.tensor_tensor(out, a, b, op).then_inc(dve_s, DV.one(name))

            def stt(name, out, a, s, b, op0=ALU.mult, op1=ALU.mult):
                return nc.vector.scalar_tensor_tensor(out=out, in0=a, scalar=s, in1=b, op0=op0, op1=op1)\
                    .then_inc(dve_s, DV.one(name))

            def norm(n, i, src, out, col, hdst):
                dve.wait_ge(pe_s, PE.at(n + "_mean", i))
                tt(n + "_xc", xc, src, bc2(bank(7)), ALU.subtract)
                dve.wait_ge(act_s, AC.at(n + "_rstd", i))
                tt(n + "_xn", out, xc, bc2(rs[:, 0, :]), ALU.mult)
                if col is None:
                    return
                tt(n + "_v1", rs[:, 1, :], bank(6), rs[:, 0, :], ALU.mult)
                dve.wait_ge(dve_s, DV.at(n + "_v1", i))
                tt(n + "_v2", rs[:, 1, :], rs[:, 1, :], rs[:, 0, :], ALU.mult)
                dve.wait_ge(act_s, AC.at(n + "_rrms", i))
                dve.wait_ge(dve_s, DV.at(n + "_xn", i))
                for c in range(DC):
                    stt(f"{n}_h{c}", hdst[:, c, :], out[:, c, :], cols[:, col + c:col + c + 1], rs[:, 1, :])

            dve.wait_ge(s_whi, 1)
            nc.vector.tensor_tensor(w_lo[:], w_in[:], w_hi[:].bitcast(F32), ALU.subtract).then_inc(s_wlo, 1)
            dve.wait_ge(s_wlo, 1)
            dve.sem_inc(dve_s, DV.per)
            with dve.Fori(0, NB) as i:
                dve.wait_ge(s_x[0], (i + 1) * 16)
                norm("in", i, x[:], xn[:], 0, h)
                dve.wait_ge(act_s, AC.at("in_hi", i))
                tt("in_lo", hlo[:], h[:], hhi[:].bitcast(F32), ALU.subtract)
                dve.wait_ge(act_s, AC.at("abs", i))
                nc.vector.tensor_scalar(lb[:], bank(7), cols[:, 6:7], 0.0, ALU.add, ALU.min).then_inc(dve_s, DV.one("zmin"))
                dve.wait_ge(act_s, AC.at("ln", i))
                dve.wait_ge(dve_s, DV.at("zmin", i))
                tt("graw", lb[:], lb[:], la[:], ALU.subtract)
                dve.wait_ge(dve_s, DV.at("graw", i))
                nc.vector.tensor_tensor_scan(cum[:], notfirst[:], lb[:], 0.0, ALU.mult, ALU.add)\
                    .then_inc(dve_s, DV.one("cum"))
                dve.wait_ge(dve_s, DV.at("cum", i))
                cum3 = cum[:].rearrange("p (c t) -> p c t", c=NCH)
                tt("dcum", lb[:].rearrange("p (c t) -> p c t", c=NCH), cum3[:, :, 63:64].broadcast_to([P, NCH, 64]),
                   cum3, ALU.subtract)
                dve.wait_ge(act_s, AC.at("eb", i))
                stt("qe", qe[:], bank(0), 16 ** -0.5, eb[:])
                dve.wait_ge(act_s, AC.at("enb", i))
                tt("ke", ke[:], bank(1), ke[:], ALU.mult)
                dve.wait_ge(act_s, AC.at("edk", i))
                tt("kd", lb[:], bank(1), lb[:], ALU.mult)
                dve.wait_ge(dve_s, DV.at("qe", i))
                for c in range(NCH):
                    tt(f"qbd{c}", qbd[:, c], qe[:, c * 64:c * 64 + 64].unsqueeze(1).broadcast_to([P, 8, 64]),
                       hmask[:].unsqueeze(2).broadcast_to([P, 8, 64]), ALU.mult)
                dve.wait_ge(pe_s, PE.at("dS", i))
                bm = bmask[:].rearrange("p a b -> p (a b)").unsqueeze(1).broadcast_to([P, 2, D])
                for k in range(4):
                    tt(f"dsm{k}", dsm[:, k], psum[:, (0, 1, 5, 6)[k], :].rearrange("p (a n) -> p a n", a=2), bm, ALU.mult)
                for c in range(8):
                    p, r, b, t = c // 2, c % 2, c // 4, c % 4
                    dve.wait_ge(dve_s, DV.at(f"S{c - 1}" if c else "dsm3", i))
                    stt(f"S{c}", S[:, b, t + 1, :], S[:, b, t, :], eb[:, c * 64 + 63:c * 64 + 64],
                        dsm[:, 2 * r + p // 2, p % 2, :], ALU.mult, ALU.add)
                for p in range(4):
                    dve.wait_ge(pe_s, PE.at(f"A{p}", i))
                    tt(f"atm{p}", atm[:, p], psum[:, 3 + p % 2, :].rearrange("p (h i) -> p h i", h=8),
                       tri[:].unsqueeze(1).broadcast_to([P, 8, 64]), ALU.mult)
                dve.wait_ge(act_s, AC.at("ro", i))
                for half in range(2):
                    tt(f"og{half}", h[:, half, :].rearrange("p (a r t) -> p r a t", a=4, r=2), o_view(half),
                       rs[:, half, :].rearrange("p (a r t) -> p r a t", a=4, r=2), ALU.mult)
                dve.wait_ge(dve_s, DV.at("og1", i))
                stt("og", h[:], h[:], cols[:, 7:8], sg[:])
                dve.wait_ge(act_s, AC.at("oghi", i))
                tt("oglo", hlo[:], h[:], hhi[:].bitcast(F32), ALU.subtract)
                dve.wait_ge(pe_s, PE.at("wo", i))
                tt("xa", xn[:], xn[:], bank(3, 2), ALU.add)
                dve.wait_ge(act_s, AC.at("r2", i))
                dve.wait_ge(dve_s, DV.at("xa", i))
                for c in range(DC):
                    stt(f"h2{c}", h[:, c, :], xn[:, c, :], cols[:, 2 + c:3 + c], rs[:, 1, :])
                dve.wait_ge(act_s, AC.at("h2hi", i))
                tt("h2lo", hlo[:], h[:], hhi[:].bitcast(F32), ALU.subtract)
                for j in range(6):
                    dve.wait_ge(act_s, AC.at(f"silu{j}", i))
                    tt(f"act{j}", af[j % 2][:], sg[:, j % 2, :], bank((1, 6)[j % 2]), ALU.mult)
                    dve.wait_ge(act_s, AC.at(f"acthi{j}", i))
                    tt(f"actlo{j}", a_lo[j % 2][:], af[j % 2][:], a_hi[j % 2][:].bitcast(F32), ALU.subtract)
                dve.wait_ge(pe_s, PE.at("down5", i))
                tt("xb", xn[:], xn[:], bank(3, 2), ALU.add)
                nc.vector.tensor_copy(S[:, :, 0, :], S[:, :, 4, :]).then_inc(dve_s, DV.one("carry"))
                dve.wait_ge(dve_s, DV.at("xb", i))
                norm("out", i, xn[:], xn[:], None, None)
                dve.wait_ge(dve_s, DV.at("out_xn", i))
                tt("x1", h[:], xn[:], x[:], ALU.add)
                dve.wait_ge(dve_s, DV.at("x1", i))
                norm("next", i, h[:], keep["y"][:, :, bass.ds(i * BT, BT)], 4, sq)
                dve.wait_ge(act_s, AC.at("next_hi", i))
                dve.wait_ge(s_x1, (i + 1) * 16)
                tt("next_lo", keep["xx_lo"][:, :, bass.ds(i * BT, BT)], sq,
                   keep["xx_hi"][:, :, bass.ds(i * BT, BT)].bitcast(F32), ALU.subtract)



def attention_layer(nc, ctx, sb, sem, psum, keep, dram):
    SCALE = float(QHD) ** -0.5
    HP = HEADS // 2
    st = ExitStack()
    with st:
        def tb(name, shape, dt=F32):
            return st.enter_context(nc.sbuf_tensor(name, shape, dt))

        def asem(name):
            return sem("attn_" + name)

        KINDS = "qkvo"
        w_in = tb("aw_in", [P, 2, 256])
        w_hi = {k: tb(f"aw_{k}hi", [P, 2, 256], F32R) for k in KINDS}
        w_lo = {k: tb(f"aw_{k}lo", [P, 2, 256], F32R) for k in KINDS}
        qk_hi = [tb(f"a_qkhi{u}", [P, 2, 1024], F32R) for u in range(2)]
        qk_lo = [tb(f"a_qklo{u}", [P, 2, 1024], F32R) for u in range(2)]
        v_hi = [tb(f"a_vhi{b}", [P, 8, 256], F32R) for b in range(2)]
        v_lo = [tb(f"a_vlo{b}", [P, 8, 256], F32R) for b in range(2)]
        prob0, prob = tb("a_probfirst", [P, P]), [tb(f"a_prob{k}", [P, 1024]) for k in range(3)]
        pt_hi = [tb(f"a_pthi{g}", [P, 4 + 4 * g, 512], F32R) for g in range(2)]
        pt_lo = [tb(f"a_ptlo{g}", [P, 4 + 4 * g, 512], F32R) for g in range(2)]
        o_hi = [tb(f"a_ohi{h}", [P, 2, 512], F32R) for h in range(2)]
        o_lo = [tb(f"a_olo{h}", [P, 2, 512], F32R) for h in range(2)]
        nmx, tot, inv = (tb(f"a_{n}", [P, 2]) for n in ("nmx", "tot", "inv"))
        S = [psum[:, 0:2, :].rearrange("p a n -> p (a n)"), psum[:, 2:4, :].rearrange("p a n -> p (a n)")]
        T = [psum[:, 4, :], psum[:, 5, :]]
        O = psum[:, 6, :]
        J = psum[:, 7, :]
        ident = keep["ident"]
        xx = (keep["xx_hi"], keep["xx_lo"])

        def xcols(k, c, b, g):
            return xx[k][:, c, :].rearrange("p (j b t) -> p j b t", j=4, b=2)[:, 2 * g:2 * g + 2, b, :]

        def xtile(k, c, b, t):
            at = (t // 2) * 512 + b * 256 + (t % 2) * P
            return xx[k][:, c, at:at + P]

        def probs(s):
            u, t = divmod(s, 8)
            return prob0 if t == 0 else prob[((0, 1, 2, 1)[u] + t - 1) % 3]

        def turn_parts(s):
            return 1 + (s % 8 >= 4)

        tb_index, n = {}, 0
        for s in range(32):
            for part in range(turn_parts(s)):
                tb_index[s, part] = n
                n += 1
        assert n % 2 == 0

        def at_step(s, later):
            return (s + later) % 32, (s + later) // 32

        QK_AT, REST_AT = (0, 1, 3, 4), (2, 5, 6, 7)
        SPLIT_AT = {8: ("o", 0), 16: ("v", 1), 21: ("q", 1), 23: ("k", 1)}
        pe_plan, act_plan, dve_plan = [], [], []
        for s in range(32):
            u, t = divmod(s, 8)
            if t in QK_AT:
                j_use, j_sh = ("qk", (u + 1) % 4, QK_AT.index(t)), int(u == 3)
            elif u % 2:
                j_use, j_sh = ("v", (u + 1) % 4 // 2, REST_AT.index(t)), int(u == 3)
            else:
                k = REST_AT.index(t)
                j_use, j_sh = ("oproj", (u // 2 - 1) % 2, k // 2, k % 2), -int(u == 0)
            pv = {6: ((u, 0), 0), 2: (((u - 1) % 4, 1), -int(u == 0))}.get(t)
            s2, sh2 = at_step(s, 2)
            s1, sh1 = at_step(s, 1)
            sm1, shm1 = at_step(s, -1)
            sm2, shm2 = at_step(s, -2)
            pe_plan.append((j_use, j_sh))
            if pv:
                pe_plan.append((("pv",) + pv[0], pv[1]))
            pe_plan.append((("score", s2), sh2))
            pe_plan += [(("turn", sm1, part), shm1) for part in range(turn_parts(sm1))]
            act_plan.append((("exp", s), 0))
            act_plan += [(("turnhi", sm2, part), shm2) for part in range(turn_parts(sm2))]
            dve_plan += [((w, s1), sh1) for w in ("mask", "max")]
            dve_plan += [(("inv", s), 0), (("norm", s), 0)]
            dve_plan += [(("turnlo", sm2, part), shm2) for part in range(turn_parts(sm2))]
            if j_use[0] == "oproj":
                dve_plan.append((("add",) + j_use[1:], j_sh))
            else:
                act_plan.append(((j_use[0] + "hi",) + j_use[1:], j_sh))
                dve_plan.append(((j_use[0] + "lo",) + j_use[1:], j_sh))
            if pv:
                act_plan.append((("ohi",) + pv[0], pv[1]))
                dve_plan.append((("olo",) + pv[0], pv[1]))
            if s in SPLIT_AT:
                act_plan.append((("w", SPLIT_AT[s][0], "hi"), SPLIT_AT[s][1]))
                dve_plan.append((("w", SPLIT_AT[s][0], "lo"), SPLIT_AT[s][1]))
        PE, AC, DV = (Steps([x for x, _ in p]) for p in (pe_plan, act_plan, dve_plan))
        shift = {**dict(pe_plan), **dict(act_plan), **dict(dve_plan)}
        pe_s, act_s, dve_s = asem("tensor_steps"), asem("scalar_steps"), asem("vector_steps")
        s_win = {k: asem(f"weights_{k}_loaded") for k in KINDS}
        s_zero, s_pad = asem("zeros"), asem("padding")

        def at(steps, name, i, of=None):
            return steps.at(name, i + (shift[of] - shift[name] if of else 0))

        def done_for(name, of):
            return name, shift[of] - shift[name]

        J_USERS = [x for x, _ in pe_plan if x[0] in ("qk", "v", "oproj")]

        def j_reader(name):
            if name[0] == "qk":
                return ("qklo",) + name[1:]
            if name[0] == "v":
                return ("vlo",) + name[1:]
            return ("add",) + name[1:]

        def run(eng, s, plan, steps, i, kind, work):
            lo, hi = {"before": (-1, -1), "first": (0, 0), "middle": (1, HP - 2), "last": (HP - 1, HP - 1),
                      "after": (HP, HP)}[kind]
            skipped = 0
            for k, (name, sh) in enumerate(plan):
                if lo + sh < 0 or hi + sh >= HP:
                    assert kind != "middle"
                    skipped += 1
                    steps.one(name)
                    continue
                if skipped:
                    if k - skipped + (i + 1) * steps.per:
                        eng.wait_ge(s, k - skipped + (i + 1) * steps.per)
                    eng.sem_inc(s, skipped)
                    skipped = 0
                work(name, i).then_inc(s, steps.one(name))
            if skipped and kind != "after":
                if k + 1 - skipped + (i + 1) * steps.per:
                    eng.wait_ge(s, k + 1 - skipped + (i + 1) * steps.per)
                eng.sem_inc(s, skipped)

        def everywhere(eng, s, plan, steps, work):
            run(eng, s, plan, steps, -1, "before", work)
            run(eng, s, plan, steps, 0, "first", work)
            with eng.Fori(1, HP - 1) as i:
                run(eng, s, plan, steps, i, "middle", work)
            run(eng, s, plan, steps, HP - 1, "last", work)
            run(eng, s, plan, steps, HP, "after", work)

        block = st.enter_context(nc.Block())

        @block.sync
        def _(sp):
            def load(k, pair, before):
                if before is not None:
                    sp.wait_ge(*before)
                sp.dma_start(w_in[:], dram["aw_" + k][:, pair]).then_inc(s_win[k], 16)

            def split(k, i):
                return dve_s, DV.at(("w", k, "lo"), i)

            load("v", 0, None)
            load("q", 0, split("v", -1))
            load("k", 0, split("q", -1))
            with sp.Fori(0, HP - 1) as i:
                load("o", i, split("k", i - 1))
                load("v", i + 1, split("o", i))
                load("q", i + 1, split("v", i))
                load("k", i + 1, split("q", i))
            load("o", HP - 1, split("k", HP - 2))

        @block.gpsimd
        def _(pool):
            nc.gpsimd.memset(prob0[:], 0.0).then_inc(s_zero, 1)

        @block.tensor
        def _(pe):
            def work(name, i):
                w = name[0]
                sh = shift[name]
                needs = []
                if w in ("qk", "v", "oproj"):
                    k = J_USERS.index(name)
                    for back in range(1, len(J_USERS)):
                        prev, turn = J_USERS[k - back], (i if k >= back else i - 1)
                        if not isinstance(i, int) or 0 <= turn + shift[prev] < HP:
                            needs.append((j_reader(prev), 0 if k >= back else -1))
                            break
                if w == "qk":
                    _, u, part = name
                    which, g, b, h = part % 2, part // 2, u // 2, u % 2
                    if part < 2:
                        needs.append(done_for(("w", "qk"[which], "lo"), name))
                    if needs:
                        pe.wait_ge(dve_s, DV.latest(i, needs))
                    for c in range(DC):
                        last = product3(nc, J, (w_hi["qk"[which]][:, c, h * P:h * P + P],
                                                w_lo["qk"[which]][:, c, h * P:h * P + P]),
                                        (xcols(0, c, b, g), xcols(1, c, b, g)), c == 0, c == 1)
                    return last
                if w == "v":
                    _, b, pair = name
                    if pair == 0:
                        needs.append(done_for(("w", "v", "lo"), name))
                    pe.wait_ge(dve_s, DV.latest(i, needs))
                    for t in range(2):
                        for c in range(DC):
                            last = product3(nc, J[:, t * 256:t * 256 + 256],
                                            (xtile(0, c, b, 2 * pair + t), xtile(1, c, b, 2 * pair + t)),
                                            (w_hi["v"][:, c, :], w_lo["v"][:, c, :]), c == 0, c == 1)
                    return last
                if w == "score":
                    s = name[1]
                    u, t = divmod(s, 8)
                    if t % 4 == 0:
                        pe.wait_ge(dve_s, at(DV, ("qklo", u, 2 * (t // 4) + 1), i, name))
                    prev, sh2 = ((s - 2, 0) if s >= 2 else (s + 30, -1))
                    if not (isinstance(i, int) and i + sh + sh2 < 0):
                        pe.wait_ge(act_s, AC.at(("exp", prev), i + sh + sh2))
                    keys = (t + 1) * P
                    cuts = [(0, min(512, max(keys, 256)))] + ([(512, max(keys, 768))] if keys > 512 else [])
                    for a, z in cuts:
                        q = [x[u % 2][:, 0, t * P:t * P + P] for x in (qk_hi, qk_lo)]
                        k = [x[u % 2][:, 1, a:z] for x in (qk_hi, qk_lo)]
                        last = product3(nc, S[s % 2][:, a:z], q, k, True, True)
                    return last
                if w == "turn":
                    _, s, part = name
                    t, n = s % 8, tb_index[s, part]
                    needs = [done_for(("norm", s), name)] if part == 0 else []
                    of, n2 = next(k for k in tb_index.items() if k[1] == (n - 2) % len(tb_index))
                    back = -int(n < 2)
                    if not (isinstance(i, int) and i + sh + back < 0):
                        lo, later = done_for(("turnlo",) + of, name)
                        needs.append((lo, later + back))
                    if needs:
                        pe.wait_ge(dve_s, DV.latest(i, needs))
                    for k in range(4 * part, min(4 * part + 4, t + 1)):
                        last = nc.tensor.transpose(T[n % 2][:, (k % 4) * P:(k % 4) * P + P],
                                                   probs(s)[:, k * P:k * P + P], ident[:])
                    return last
                if w == "pv":
                    _, u, g = name
                    b, h = u // 2, u % 2
                    needs = [done_for(("turnlo", 8 * u + 4 * g + 3, g), name), done_for(("vlo", b, 2 * g + 1), name)]
                    pu, pg, psh = (u, 0, 0) if g else ((u - 1) % 4, 1, -int(u == 0))
                    if not (isinstance(i, int) and i + sh + psh < 0):
                        needs.append((("olo", pu, pg), sh + psh - shift[("olo", pu, pg)]))
                    pe.wait_ge(dve_s, DV.latest(i, needs))
                    for kt in range(4 * g + 4):
                        off = min(max(0, kt - 4 * g) * P, 256)
                        vv = [x[b][:, kt, h * P:h * P + P] for x in (v_hi, v_lo)]
                        pp = [x[g][:, kt, off:512] for x in (pt_hi, pt_lo)]
                        last = product3(nc, O[:, off:512], vv, pp, kt == 0, kt == 4 * g + 3)
                    return last
                _, b, g, m = name
                needs += [done_for(("olo", 2 * b + 1, g), name), done_for(("w", "o", "lo"), name)]
                pe.wait_ge(dve_s, DV.latest(i, needs))
                for h in range(2):
                    last = product3(nc, J, (w_hi["o"][:, h, m * P:m * P + P], w_lo["o"][:, h, m * P:m * P + P]),
                                    (o_hi[h][:, g, :], o_lo[h][:, g, :]), h == 0, h == 1)
                return last

            everywhere(pe, pe_s, pe_plan, PE, work)

        def turned(x, s, part):
            t = s % 8
            k0, k1 = 4 * part, min(4 * part + 4, t + 1)
            return x[t // 4][:, k0:k1, (t % 4) * P:(t % 4) * P + P], T[tb_index[s, part] % 2][:, 0:(k1 - k0) * P]\
                .rearrange("p (k n) -> p k n", n=P)

        @block.scalar
        def _(act):
            def work(name, i):
                w = name[0]
                if w == "w":
                    k = name[1]
                    act.wait_ge(s_win[k], (i + shift[name] + 1) * 16)
                    if not (isinstance(i, int) and i + shift[name] == 0):
                        last_use = {"o": ("oproj", 1, 1, 1), "v": ("v", 1, 3)}.get(k, ("qk", 3, 3))
                        act.wait_ge(pe_s, PE.at(last_use, i))
                    return nc.scalar.activation(w_hi[k][:], w_in[:], ACT.Copy)
                if w == "qkhi":
                    _, u, part = name
                    act.wait_ge(pe_s, PE.at(("qk", u, part), i))
                    return nc.scalar.activation(qk_hi[u % 2][:, part % 2, (part // 2) * 512:(part // 2) * 512 + 512],
                                                J, ACT.Copy, scale=(SCALE, 1.0)[part % 2])
                if w == "vhi":
                    _, b, t = name
                    act.wait_ge(pe_s, PE.at(("v", b, t), i))
                    return nc.scalar.activation(v_hi[b][:, 2 * t:2 * t + 2, :].rearrange("p t n -> p (t n)"), J, ACT.Copy)
                if w == "exp":
                    s = name[1]
                    keys = (s % 8 + 1) * P
                    act.wait_ge(dve_s, at(DV, ("max", s), i, name))
                    return nc.scalar.activation(probs(s)[:, 0:keys], S[s % 2][:, 0:keys], ACT.Exp,
                                                bias=nmx[:, s % 2:s % 2 + 1],
                                                accum_out=tot[:, s % 2:s % 2 + 1])
                if w == "turnhi":
                    _, s, part = name
                    act.wait_ge(pe_s, at(PE, ("turn", s, part), i, name))
                    to, of = turned(pt_hi, s, part)
                    return nc.scalar.activation(to, of, ACT.Copy)
                _, u, g = name
                act.wait_ge(pe_s, at(PE, ("pv", u, g), i, name))
                return nc.scalar.activation(o_hi[u % 2][:, g, :], O, ACT.Copy)

            everywhere(act, act_s, act_plan, AC, work)

        @block.vector
        def _(dve):
            dve.wait_ge(s_zero, 1)
            for g in range(2):
                for x in (pt_hi, pt_lo):
                    nc.vector.tensor_copy(x[g][:, 4 * g + 3, 256:384], prob0[:]).then_inc(s_pad, 1)
            dve.wait_ge(s_pad, 4)

            def work(name, i):
                w = name[0]
                if w == "w":
                    k = name[1]
                    dve.wait_ge(act_s, at(AC, ("w", k, "hi"), i, name))
                    return nc.vector.tensor_tensor(w_lo[k][:], w_in[:],
                                                   w_hi[k][:].bitcast(F32), ALU.subtract)
                if w == "qklo":
                    _, u, part = name
                    dve.wait_ge(act_s, AC.at(("qkhi", u, part), i))
                    a = (part // 2) * 512
                    to, hi = (x[u % 2][:, part % 2, a:a + 512] for x in (qk_lo, qk_hi))
                    if part % 2 == 0:
                        return nc.vector.scalar_tensor_tensor(out=to, in0=J, scalar=SCALE, in1=hi.bitcast(F32),
                                                              op0=ALU.mult, op1=ALU.subtract)
                    return nc.vector.tensor_tensor(to, J, hi.bitcast(F32), ALU.subtract)
                if w == "vlo":
                    _, b, t = name
                    dve.wait_ge(act_s, AC.at(("vhi", b, t), i))
                    to, hi = (x[b][:, 2 * t:2 * t + 2, :].rearrange("p t n -> p (t n)") for x in (v_lo, v_hi))
                    return nc.vector.tensor_tensor(to, J, hi.bitcast(F32), ALU.subtract)
                if w == "mask":
                    s = name[1]
                    t = s % 8
                    dve.wait_ge(pe_s, at(PE, ("score", s), i, name))
                    x = S[s % 2][:, t * P:t * P + P]
                    return nc.vector.tensor_tensor(x, x, keep["cmask"][:], ALU.add)
                if w == "max":
                    s = name[1]
                    dve.wait_ge(dve_s, DV.at(("mask", s), i))
                    return nc.vector.tensor_reduce(nmx[:, s % 2:s % 2 + 1], S[s % 2][:, 0:(s % 8 + 1) * P], AX_X,
                                                   ALU.max, negate=True)
                if w == "turnlo":
                    _, s, part = name
                    dve.wait_ge(act_s, at(AC, ("turnhi", s, part), i, name))
                    to, of = turned(pt_lo, s, part)
                    hi, _ = turned(pt_hi, s, part)
                    return nc.vector.tensor_tensor(to, of, hi.bitcast(F32), ALU.subtract)
                if w == "inv":
                    s = name[1]
                    dve.wait_ge(act_s, AC.at(("exp", s), i))
                    return nc.vector.reciprocal(inv[:, s % 2:s % 2 + 1], tot[:, s % 2:s % 2 + 1])
                if w == "norm":
                    s = name[1]
                    dve.wait_ge(dve_s, DV.at(("inv", s), i))
                    x = probs(s)[:, 0:(s % 8 + 1) * P]
                    return nc.vector.tensor_scalar(x, x, inv[:, s % 2:s % 2 + 1], None, ALU.mult)
                if w == "olo":
                    _, u, g = name
                    dve.wait_ge(act_s, at(AC, ("ohi", u, g), i, name))
                    return nc.vector.tensor_tensor(o_lo[u % 2][:, g, :], O, o_hi[u % 2][:, g, :].bitcast(F32),
                                                   ALU.subtract)
                _, b, g, m = name
                dve.wait_ge(pe_s, at(PE, ("oproj",) + name[1:], i, name))
                y = keep["y"][:, m, :].rearrange("p (j b t) -> p j b t", j=4, b=2)[:, 2 * g:2 * g + 2, b, :]
                return nc.vector.tensor_tensor(y, y, J.rearrange("p (j t) -> p j t", j=2), ALU.add)

            everywhere(dve, dve_s, dve_plan, DV, work)


def router(nc, ctx, sb, sem, psum, keep, dram):
    st = ExitStack()
    with st:
        def tb(name, shape, dt=F32):
            return st.enter_context(nc.sbuf_tensor(name, shape, dt))

        def rsem(name):
            return sem("route_" + name)

        E, TOPK, TT = 16, 4, 16
        ones, gw, col = tb("r_ones", [P, P]), tb("r_gw", [P, DC, E]), tb("r_col", [P, DC])
        sq, rs, x2 = tb("r_sq", [P, DC, BT]), tb("r_rs", [P, BT]), tb("r_x2", [P, DC, BT])
        lg, pr, q, eq, sel = (tb(f"r_{n}", [P, TT, E]) for n in ("lg", "pr", "q", "eq", "sel"))
        rank = tb("r_rank", [P, E])
        m1, m2 = tb("r_m1", [P, TT]), tb("r_m2", [P, TT])
        wfT = tb("r_wfT", [P, 2, P])
        s_in, s_const, s_out = rsem("loaded"), rsem("constants"), rsem("weights_stored")
        pe_s, act_s, dve_s = rsem("tensor_steps"), rsem("scalar_steps"), rsem("vector_steps")
        s_gate, s_exp, s_turn, s_turned = rsem("gating"), rsem("exponentials"), rsem("turned"), rsem("turned_copied")
        PE = Steps(["ms", "logits"])
        AC = Steps(["sq", "ln", "r", "hi", "logits"])
        DV = Steps(["x20", "x21", "lo"])
        GATED = 6 + 6 * TOPK + 4

        block = st.enter_context(nc.Block())

        @block.sync
        def _(sp):
            sp.dma_start(gw[:], dram["gate_w"]).then_inc(s_in, 16)
            sp.dma_start(col[:], dram["cols2"]).then_inc(s_in, 16)
            sp.wait_ge(s_turned, 1)
            for g in range(2):
                for t in range(8):
                    sp.dma_start(dram["route"][:, (8 * g + t) * P:(8 * g + t + 1) * P],
                                 wfT[16 * t:16 * t + 16, g, :]).then_inc(s_out, 16)
            sp.wait_ge(s_out, 16 * 16)

        @block.gpsimd
        def _(pool):
            nc.gpsimd.memset(ones[:], 1.0 / D).then_inc(s_const, 1)
            for e in range(E):
                nc.gpsimd.memset(rank[:, e:e + 1], float(E - e)).then_inc(s_const, 1)

        @block.tensor
        def _(pe):
            pe.wait_ge(s_const, 1 + E)
            pe.wait_ge(s_in, 32)
            pe.sem_inc(pe_s, PE.per)
            with pe.Fori(0, NB) as i:
                pe.wait_ge(act_s, AC.at("sq", i))
                for c in range(DC):
                    last = nc.tensor.matmul(psum[:, 7, :], ones[:], sq[:, c, :], start=c == 0, stop=c == 1)
                last.then_inc(pe_s, PE.one("ms"))
                pe.wait_ge(dve_s, DV.at("x21", i))
                pe.wait_ge(act_s, AC.at("logits", i - 1))
                for t in range(4):
                    for c in range(DC):
                        last = nc.tensor.matmul(psum[:, 6, t * E:t * E + E], x2[:, c, t * P:t * P + P], gw[:, c, :],
                                                start=c == 0, stop=c == 1)
                last.then_inc(pe_s, PE.one("logits"))
            pe.wait_ge(s_gate, GATED)
            for g in range(2):
                last = nc.tensor.transpose(psum[:, 5, g * P:g * P + P],
                                           q[:, 8 * g:8 * g + 8, :].rearrange("p t e -> p (t e)"), keep["ident"][:])
            last.then_inc(s_turn, 1)

        @block.scalar
        def _(act):
            act.wait_ge(s_const, 1)
            act.sem_inc(act_s, AC.per)
            with act.Fori(0, NB) as i:
                act.wait_ge(pe_s, PE.at("ms", i - 1))
                nc.scalar.activation(sq[:], keep["y"][:, :, bass.ds(i * BT, BT)], ACT.Square).then_inc(act_s, AC.one("sq"))
                act.wait_ge(pe_s, PE.at("ms", i))
                act.wait_ge(dve_s, DV.at("x21", i - 1))
                nc.scalar.activation(rs[:], psum[:, 7, :], ACT.Ln, bias=keep["eps"][:, 1:2]).then_inc(act_s, AC.one("ln"))
                act.wait_ge(act_s, AC.at("ln", i))
                nc.scalar.activation(rs[:], rs[:], ACT.Exp, scale=-0.5).then_inc(act_s, AC.one("r"))
                act.wait_ge(dve_s, DV.at("x21", i))
                nc.scalar.activation(keep["xx_hi"][:, :, bass.ds(i * BT, BT)], x2[:], ACT.Copy)\
                    .then_inc(act_s, AC.one("hi"))
                act.wait_ge(pe_s, PE.at("logits", i))
                nc.scalar.activation(lg[:].rearrange("p t e -> p (t e)")[:, bass.ds(i * 4 * E, 4 * E)],
                                     psum[:, 6, 0:4 * E], ACT.Copy).then_inc(act_s, AC.one("logits"))
            act.wait_ge(s_gate, 2)
            nc.scalar.activation(pr[:], lg[:], ACT.Exp).then_inc(s_exp, 1)
            act.wait_ge(s_turn, 1)
            nc.scalar.activation(wfT[:].rearrange("p g n -> p (g n)"), psum[:, 5, 0:2 * P], ACT.Copy).then_inc(s_turned, 1)

        @block.vector
        def _(dve):
            dve.wait_ge(s_in, 32)
            dve.wait_ge(s_const, 1 + E)
            dve.sem_inc(dve_s, DV.per)
            with dve.Fori(0, NB) as i:
                dve.wait_ge(act_s, AC.at("r", i))
                dve.wait_ge(pe_s, PE.at("logits", i - 1))
                dve.wait_ge(dve_s, DV.at("lo", i - 1))
                for c in range(DC):
                    nc.vector.scalar_tensor_tensor(out=x2[:, c, :], in0=keep["y"][:, c, bass.ds(i * BT, BT)],
                                                   scalar=col[:, c:c + 1], in1=rs[:], op0=ALU.mult, op1=ALU.mult)\
                        .then_inc(dve_s, DV.one(f"x2{c}"))
                dve.wait_ge(act_s, AC.at("hi", i))
                nc.vector.tensor_tensor(keep["xx_lo"][:, :, bass.ds(i * BT, BT)], x2[:],
                                        keep["xx_hi"][:, :, bass.ds(i * BT, BT)].bitcast(F32), ALU.subtract)\
                    .then_inc(dve_s, DV.one("lo"))
            n = [0]

            def link(ins):
                n[0] += 1
                ins.then_inc(s_gate, 1)
                dve.wait_ge(s_gate, n[0])

            def wide(ap):
                return ap.unsqueeze(2).broadcast_to([P, TT, E])

            dve.wait_ge(act_s, AC.at("logits", NB - 1))
            link(nc.vector.reduce_max(m1[:], lg[:], AX_X))
            link(nc.vector.tensor_tensor(lg[:], lg[:], wide(m1[:]), ALU.subtract))
            dve.wait_ge(s_exp, 1)
            link(nc.vector.reduce_sum(m1[:], pr[:], AX_X))
            link(nc.vector.reciprocal(m2[:], m1[:]))
            link(nc.vector.tensor_tensor(pr[:], pr[:], wide(m2[:]), ALU.mult))
            link(nc.vector.tensor_copy(q[:], pr[:]))
            rk = rank[:].unsqueeze(1).broadcast_to([P, TT, E])
            for _ in range(TOPK):
                link(nc.vector.reduce_max(m1[:], q[:], AX_X))
                link(nc.vector.tensor_tensor(eq[:], q[:], wide(m1[:]), ALU.is_equal))
                link(nc.vector.tensor_tensor(eq[:], eq[:], rk, ALU.mult))
                link(nc.vector.reduce_max(m2[:], eq[:], AX_X))
                link(nc.vector.tensor_tensor(sel[:], eq[:], wide(m2[:]), ALU.is_equal))
                link(nc.vector.scalar_tensor_tensor(out=q[:], in0=sel[:], scalar=-4.0, in1=q[:], op0=ALU.mult, op1=ALU.add))
            link(nc.vector.scalar_tensor_tensor(out=q[:], in0=q[:], scalar=-1.0, in1=pr[:], op0=ALU.is_lt, op1=ALU.mult))
            link(nc.vector.reduce_sum(m1[:], q[:], AX_X))
            link(nc.vector.reciprocal(m2[:], m1[:]))
            link(nc.vector.tensor_tensor(q[:], q[:], wide(m2[:]), ALU.mult))
            assert n[0] == GATED


def experts(nc, ctx, sb, sem, psum, keep, dram):
    st = ExitStack()
    with st:
        def tb(name, shape, dt=F32):
            return st.enter_context(nc.sbuf_tensor(name, shape, dt))

        def esem(name):
            return sem("moe_" + name)

        N, HALF, ITER = 24, 12, PAIRS // 2
        w_in = tb("e_win", [P, 3, 768])
        w_hi = [tb(f"e_whi{k}", [P, 3, 768], F32R) for k in range(2)]
        w_lo = [tb(f"e_wlo{k}", [P, 3, 768], F32R) for k in range(2)]
        share = [tb(f"e_share{k}", [P, 3, NB * BT]) for k in range(2)]
        sg = [tb(f"e_sg{k}", [P, BT]) for k in range(2)]
        a1 = [tb(f"e_a1{k}", [P, BT]) for k in range(2)]
        af = [tb(f"e_af{k}", [P, BT]) for k in range(2)]
        ahi = [tb(f"e_ahi{k}", [P, BT], F32R) for k in range(2)]
        alo = [tb(f"e_alo{k}", [P, BT], F32R) for k in range(2)]
        G, U, DN = (lambda n: psum[:, n % 3, :]), (lambda n: psum[:, 3 + n % 3, :]), psum[:, 6:8, :]

        pe_plan, act_plan, dve_plan = [], [], []
        for n in range(N):
            pe_plan += [(("gu", (n + 2) % N), (n + 2) // N), (("down", n), 0)]
            w = {4: (1, 0, 0), 5: (1, 1, 0), 6: (1, 2, 0), 16: (0, 0, 1), 17: (0, 1, 1), 18: (0, 2, 1)}.get(n)
            act_plan += [(("silu", (n + 1) % N), (n + 1) // N), (("hi", n), 0)]
            if n % 3 == 0:
                dve_plan.append((("add", (n - 1) % N), -int(n == 0)))
            dve_plan += [(("weigh", (n + 1) % N), (n + 1) // N), (("act", (n + 1) % N), (n + 1) // N), (("lo", n), 0)]
            if w:
                act_plan.append((("w", w[0], w[1], "hi"), w[2]))
                dve_plan.append((("w", w[0], w[1], "lo"), w[2]))
        PE, AC, DV = (Steps([x for x, _ in p]) for p in (pe_plan, act_plan, dve_plan))
        shift = {**dict(pe_plan), **dict(act_plan), **dict(dve_plan)}
        pe_s, act_s, dve_s = esem("tensor_steps"), esem("scalar_steps"), esem("vector_steps")
        s_w, s_share, s_one = esem("weights_loaded"), [esem(f"share{k}_loaded") for k in range(2)], esem("share_one")

        def at(steps, name, i, of=None):
            return steps.at(name, i + (shift[of] - shift[name] if of else 0))

        def done_for(name, of):
            return name, shift[of] - shift[name]

        def pair_of(name, i):
            q = name[1] if name[0] == "w" else name[1] // HALF
            return 2 * (i + shift[name]) + 1 + q

        def run(eng, s, plan, steps, i, work):
            known = isinstance(i, int)
            skipped = 0
            for k, (name, sh) in enumerate(plan):
                if known and not 0 <= pair_of(name, i) < PAIRS:
                    skipped += 1
                    steps.one(name)
                    continue
                if skipped:
                    if k - skipped + (i + 1) * steps.per:
                        eng.wait_ge(s, k - skipped + (i + 1) * steps.per)
                    eng.sem_inc(s, skipped)
                    skipped = 0
                work(name, i).then_inc(s, steps.one(name))
            if skipped and i != ITER:
                eng.wait_ge(s, k + 1 - skipped + (i + 1) * steps.per)
                eng.sem_inc(s, skipped)

        def everywhere(eng, s, plan, steps, work):
            run(eng, s, plan, steps, -1, work)
            with eng.Fori(0, ITER - 1) as i:
                run(eng, s, plan, steps, i, work)
            run(eng, s, plan, steps, ITER - 1, work)
            run(eng, s, plan, steps, ITER, work)

        def before(name, back, i):
            n = name[1] - back
            d = -int(n < 0)
            if isinstance(i, int) and 2 * (i + shift[name] + d) + 1 + (n % N) // HALF < 0:
                return None
            return n % N, d

        block = st.enter_context(nc.Block())

        @block.sync
        def _(sp):
            sp.dma_start(w_in[:], dram["moe_w"][:, 0]).then_inc(s_w, 16)
            sp.wait_ge(s_one, 2)
            with sp.Fori(0, ITER) as i:
                for q in range(2):
                    sp.wait_ge(dve_s, DV.at(("w", 1 - q, 2, "lo"), i - 1))
                    sp.dma_start(w_in[:], dram["moe_w"][:, bass.ds(2 * i + 1 + q, 1)].rearrange("p a c n -> p (a c) n"))\
                        .then_inc(s_w, 16)
                    sp.wait_ge(dve_s, DV.at(("weigh", 11 + 12 * q), i - 1 + (0 if q == 0 else 0)))
                    for e in range(2):
                        row = dram["route"][bass.ds(4 * i + 2 * q + e, 1), :]
                        sp.dma_start(share[q][:, e, :], row.broadcast_to([P, NB * BT])).then_inc(s_share[q], 16)
                        sp.dma_start(share[q][48 * e:48 * e + 48, 2, :], row.broadcast_to([48, NB * BT]))\
                            .then_inc(s_share[q], 16)

        @block.gpsimd
        def _(pool):
            for q in range(2):
                nc.gpsimd.memset(share[q][:], 1.0).then_inc(s_one, 1)

        @block.tensor
        def _(pe):
            def work(name, i):
                n = name[1]
                q, t, j = n // HALF, (n % HALF) // 3, n % 3
                needs = []
                if name[0] == "gu":
                    if n % HALF == 0:
                        needs.append(done_for(("w", q, 1, "lo"), name))
                    p = before(name, 3, i)
                    if p:
                        done, later = done_for(("act", p[0]), name)
                        needs.append((done, later + p[1]))
                    if needs:
                        pe.wait_ge(dve_s, DV.latest(i, needs))
                    for g, out in enumerate((G(n), U(n))):
                        for c in range(DC):
                            o = g * 384 + j * P
                            last = product3(nc, out, (w_hi[q][:, c, o:o + P], w_lo[q][:, c, o:o + P]),
                                            (keep["xx_hi"][:, c, t * BT:t * BT + BT], keep["xx_lo"][:, c, t * BT:t * BT + BT]),
                                            c == 0, c == 1)
                    return last
                needs = [done_for(("lo", n), name)]
                if n % HALF == 0:
                    needs.append(done_for(("w", q, 2, "lo"), name))
                if j == 0:
                    p = before(name, 1, i)
                    if p:
                        add, later = done_for(("add", p[0]), name)
                        needs.append((add, later + p[1]))
                pe.wait_ge(dve_s, DV.latest(i, needs))
                for m in range(2):
                    o = j * D + m * P
                    last = product3(nc, DN[:, m, :], (w_hi[q][:, 2, o:o + P], w_lo[q][:, 2, o:o + P]),
                                    (ahi[n % 2][:], alo[n % 2][:]), j == 0, j == 2)
                return last

            everywhere(pe, pe_s, pe_plan, PE, work)

        @block.scalar
        def _(act):
            def work(name, i):
                if name[0] == "w":
                    _, q, part, _ = name
                    if part == 0:
                        act.wait_ge(s_w, (pair_of(name, i) + 1) * 16)
                        if not (isinstance(i, int) and pair_of(name, i) < 2):
                            act.wait_ge(pe_s, PE.at(("down", 12 * q + 11), i + shift[name] - 1))
                    return nc.scalar.activation(w_hi[q][:, part, :], w_in[:, part, :], ACT.Copy)
                n = name[1]
                if name[0] == "silu":
                    act.wait_ge(pe_s, at(PE, ("gu", n), i, name))
                    return nc.scalar.activation(sg[n % 2][:], G(n), ACT.Silu)
                act.wait_ge(dve_s, at(DV, ("act", n), i, name))
                p = before(name, 2, i)
                if p:
                    act.wait_ge(pe_s, at(PE, ("down", p[0]), i + p[1], name))
                return nc.scalar.activation(ahi[n % 2][:], af[n % 2][:], ACT.Copy)

            everywhere(act, act_s, act_plan, AC, work)

        @block.vector
        def _(dve):
            dve.wait_ge(s_one, 2)

            def work(name, i):
                if name[0] == "w":
                    _, q, part, _ = name
                    dve.wait_ge(act_s, at(AC, ("w", q, part, "hi"), i, name))
                    return nc.vector.tensor_tensor(w_lo[q][:, part, :], w_in[:, part, :],
                                                   w_hi[q][:, part, :].bitcast(F32), ALU.subtract)
                n = name[1]
                q, t, j = n // HALF, (n % HALF) // 3, n % 3
                if name[0] == "weigh":
                    act_done = at(PE, ("gu", n), i, name)
                    dve.wait_ge(pe_s, act_done)
                    if n % HALF == 0 and not (isinstance(i, int) and pair_of(name, i) == 0):
                        dve.wait_ge(s_share[q], (i + shift[name] + 1) * 64)
                    return nc.vector.tensor_tensor(a1[n % 2][:], U(n), share[q][:, j, t * BT:t * BT + BT], ALU.mult)
                if name[0] == "act":
                    dve.wait_ge(dve_s, at(DV, ("weigh", n), i, name))
                    dve.wait_ge(act_s, at(AC, ("silu", n), i, name))
                    return nc.vector.tensor_tensor(af[n % 2][:], a1[n % 2][:], sg[n % 2][:], ALU.mult)
                if name[0] == "lo":
                    dve.wait_ge(act_s, at(AC, ("hi", n), i, name))
                    return nc.vector.tensor_tensor(alo[n % 2][:], af[n % 2][:], ahi[n % 2][:].bitcast(F32), ALU.subtract)
                dve.wait_ge(pe_s, at(PE, ("down", n), i, name))
                y = keep["y"][:, :, t * BT:t * BT + BT]
                return nc.vector.tensor_tensor(y, y, DN, ALU.add)

            everywhere(dve, dve_s, dve_plan, DV, work)


def last_norm(nc, ctx, sb, sem, psum, keep, dram):
    st = ExitStack()
    with st:
        def tb(name, shape, dt=F32):
            return st.enter_context(nc.sbuf_tensor(name, shape, dt))

        def fsem(name):
            return sem("last_" + name)

        ones, rs = tb("f_ones", [P, P]), [tb(f"f_rs{k}", [P, BT]) for k in range(2)]
        x1 = tb("f_x1", [P, DC, NB * BT])
        xc, sq, out = ([tb(f"f_{n}{k}", [P, DC, BT]) for k in range(2)] for n in ("xc", "sq", "out"))
        s_x1 = [fsem(f"x1_loaded{b}") for b in range(NB)]
        s_one, s_mean, s_var, s_sq = fsem("ones"), fsem("mean"), fsem("variance"), fsem("squares")
        s_ln, s_r, s_xc, s_xn, s_sum = (fsem(n) for n in ("ln", "rstd", "centered", "normed", "sum"))
        s_out = [fsem(f"stored{k}") for k in range(2)]
        block = st.enter_context(nc.Block())

        def bc2(ap):
            return ap.unsqueeze(1).broadcast_to([P, DC, BT])

        @block.sync
        def _(sp):
            for b in range(NB):
                sp.dma_start(x1[:, :, b * BT:b * BT + BT], dram["x1"][:, :, b * BT:b * BT + BT]).then_inc(s_x1[b], 16)
            for b in range(NB):
                sp.wait_ge(s_sum, b + 1)
                sp.dma_start(dram["outT"][:, :, b * BT:b * BT + BT], out[b % 2][:]).then_inc(s_out[b % 2], 16)
            for k in range(2):
                sp.wait_ge(s_out[k], 16 * NB // 2)

        @block.gpsimd
        def _(pool):
            nc.gpsimd.memset(ones[:], 1.0 / D).then_inc(s_one, 1)

        @block.tensor
        def _(pe):
            pe.wait_ge(s_one, 1)

            def mean(b):
                if b >= 2:
                    pe.wait_ge(s_xc, b - 1)
                for c in range(DC):
                    last = nc.tensor.matmul(psum[:, b % 2, :], ones[:], keep["y"][:, c, b * BT:b * BT + BT],
                                            start=c == 0, stop=c == 1)
                last.then_inc(s_mean, 1)

            mean(0)
            for b in range(NB):
                if b + 1 < NB:
                    mean(b + 1)
                pe.wait_ge(s_sq, b + 1)
                if b >= 2:
                    pe.wait_ge(s_ln, b - 1)
                for c in range(DC):
                    last = nc.tensor.matmul(psum[:, 2 + b % 2, :], ones[:], sq[b % 2][:, c, :], start=c == 0, stop=c == 1)
                last.then_inc(s_var, 1)

        @block.scalar
        def _(act):
            for b in range(NB):
                act.wait_ge(s_xc, b + 1)
                nc.scalar.activation(sq[b % 2][:], xc[b % 2][:], ACT.Square).then_inc(s_sq, 1)
                act.wait_ge(s_var, b + 1)
                if b >= 2:
                    act.wait_ge(s_xn, b - 1)
                nc.scalar.activation(rs[b % 2][:], psum[:, 2 + b % 2, :], ACT.Ln, bias=keep["eps"][:, 0:1]).then_inc(s_ln, 1)
                act.wait_ge(s_ln, b + 1)
                nc.scalar.activation(rs[b % 2][:], rs[b % 2][:], ACT.Exp, scale=-0.5).then_inc(s_r, 1)

        @block.vector
        def _(dve):
            def center(b):
                dve.wait_ge(s_mean, b + 1)
                if b >= 2:
                    dve.wait_ge(s_sum, b - 1)
                nc.vector.tensor_tensor(xc[b % 2][:], keep["y"][:, :, b * BT:b * BT + BT], bc2(psum[:, b % 2, :]),
                                        ALU.subtract).then_inc(s_xc, 1)

            center(0)
            for b in range(NB):
                if b + 1 < NB:
                    center(b + 1)
                dve.wait_ge(s_r, b + 1)
                if b >= 2:
                    dve.wait_ge(s_out[b % 2], 16 * (b // 2))
                nc.vector.tensor_tensor(out[b % 2][:], xc[b % 2][:], bc2(rs[b % 2][:]), ALU.mult).then_inc(s_xn, 1)
                dve.wait_ge(s_xn, b + 1)
                dve.wait_ge(s_x1[b], 16)
                nc.vector.tensor_tensor(out[b % 2][:], out[b % 2][:], x1[:, :, b * BT:b * BT + BT], ALU.add)\
                    .then_inc(s_sum, 1)


def build(nc, dram):
    ctx = ExitStack()
    with ctx:
        def sb(name, shape, dt=F32):
            return ctx.enter_context(nc.sbuf_tensor(name, shape, dt))

        def sem(name):
            return ctx.enter_context(nc.semaphore(name))

        psum = ctx.enter_context(nc.psum_tensor("psum", [P, 8, 512], F32))
        keep = {"y": sb("y", [P, DC, NB * BT]), "xx_hi": sb("xx_hi", [P, DC, NB * BT], F32R),
                "xx_lo": sb("xx_lo", [P, DC, NB * BT], F32R), "ident": sb("ident", [P, P]),
                "cmask": sb("cmask", [P, P]), "eps": sb("eps", [P, 2])}
        gla_layer(nc, ctx, sb, sem, psum, keep, dram)
        attention_layer(nc, ctx, sb, sem, psum, keep, dram)
        router(nc, ctx, sb, sem, psum, keep, dram)
        experts(nc, ctx, sb, sem, psum, keep, dram)
        last_norm(nc, ctx, sb, sem, psum, keep, dram)


def kernel(**inputs):
    import numpy as np
    import concourse.bacc as bacc
    from concourse.bass_utils import run_bass_kernel_spmd

    a = {k: np.asarray(v) for k, v in inputs.items()}
    f = np.float32

    def rows(w):
        return w.reshape(DC, P, -1).transpose(1, 0, 2)

    def turned_tokens(x):
        return x.reshape(2, NB, 256, DC, P).transpose(4, 3, 1, 0, 2).reshape(P, DC, NB * BT)

    A, B = "L0_attn_", "L0_ffn_"
    arrays = {"xT": turned_tokens(a[A + "x"])}
    for n in ("wq", "wk", "wv", "wg", "wo", "gk_w1", "gk_w2", "w_gate", "w_up", "w_down"):
        arrays[n] = a[A + n]
    col = lambda w: w.reshape(DC, P).T
    arrays["cols"] = np.concatenate([col(a[A + "norm1_w"]), col(a[A + "ffn_norm_w"]), col(a[B + "ln1_w"]),
                                     a[A + "gk_b"][:, None], np.tile(a[A + "gnorm_w"], 4)[:, None]], axis=1)
    arrays["cols2"] = col(a[B + "ln2_w"])

    def heads(w):
        return w.reshape(8, 2, P, DC, P).transpose(4, 0, 3, 1, 2).reshape(P, 8, DC, 2 * P)

    kv = a[B + "kv_w"]
    arrays["aw_q"] = heads(a[B + "q_w"].reshape(HEADS, QHD, D)[:, :P])
    arrays["aw_k"] = heads(kv[:HEADS * P].reshape(HEADS, P, D))
    arrays["aw_v"] = heads(kv[HEADS * P:2 * HEADS * P].reshape(HEADS, P, D))
    arrays["aw_o"] = a[B + "o_w"].reshape(D, 8, 2, P).transpose(3, 1, 2, 0)
    arrays["gate_w"] = rows(a[B + "gate_w"].T)

    w = np.zeros((PAIRS, 3, P, 768), f)
    w1, w2 = a[B + "w1"], a[B + "w2"]
    I, R = w2.shape[2], w2.shape[2] - P
    sgu, sdn = a[B + "sh_gu_w"], a[B + "sh_down_w"]
    w2v = w[:, 2].reshape(PAIRS, P, 3, D)
    for g in range(2):
        w[0, 0:2, :, g * 384:g * 384 + 2 * I] = sgu[g * 2 * I:(g + 1) * 2 * I].T.reshape(DC, P, 2 * I)
        for e in range(2):
            one = w1[e::2, g * I:(g + 1) * I].transpose(0, 2, 1).reshape(8, DC, P, I)
            w[1:, 0:2, :, g * 384 + e * P:g * 384 + (e + 1) * P] = one[..., :P]
            w[1:, 0:2, :, g * 384 + 2 * P + e * R:g * 384 + 2 * P + (e + 1) * R] = one[..., P:]
    for e in range(2):
        w2v[0, :, e, :] = sdn[:, e * P:(e + 1) * P].T
        w2v[1:, :, e, :] = w2[e::2, :, :P].transpose(0, 2, 1)
        w2v[1:, e * R:(e + 1) * R, 2, :] = w2[e::2, :, P:].transpose(0, 2, 1)
    w2v[0, :2 * R, 2, :] = sdn[:, 2 * P:].T
    arrays["moe_w"] = w.transpose(2, 0, 1, 3)

    nc = bacc.Bacc("TRN2", target_bir_lowering=False, num_devices=1)
    dram, args = {}, {}
    for n, x in arrays.items():
        x = np.ascontiguousarray(x)
        args["in_" + n] = x
        dram[n] = nc.dram_tensor("in_" + n, x.shape, mybir.dt.from_np(x.dtype), kind="ExternalInput").ap()
    dram["outT"] = nc.dram_tensor("outT", (P, DC, NB * BT), F32, kind="ExternalOutput").ap()
    dram["x1"] = nc.dram_tensor("x1", (P, DC, NB * BT), F32, kind="Internal").ap()
    dram["route"] = nc.dram_tensor("route", (16, NB * BT), F32, kind="Internal").ap()
    build(nc, dram)
    r = run_bass_kernel_spmd(nc, [args], core_ids=[0])
    o = r.results[0]["outT"].reshape(P, DC, NB, 2, 256)
    return o.transpose(3, 2, 4, 1, 0).reshape(2, NB * 256, D)
```

```python
from contextlib import ExitStack

import concourse.bass as bass
from concourse import mybir

F32 = mybir.dt.float32
F32R = mybir.dt.float32r
ALU = mybir.AluOpType
ACT = mybir.ActivationFunctionType
AX_X = mybir.AxisListType.X

P = 128
D = 256
DC = D // P
NB = 4
BT = 512
HID = 6 * P
NCH = 8
EPS_LN = 1e-5
EPS_RMS = 1e-6
MASKED = -3e10
PAIRS = 9
HEADS = 16
QHD = 192


class Steps:

    def __init__(self, names):
        self.index = {n: k for k, n in enumerate(names)}
        self.names = list(names)
        self.per = len(self.names)
        self.made = 0
        assert len(self.index) == self.per

    def at(self, name, i):
        return (i + 1) * self.per + (self.index[name] + 1)

    def latest(self, i, needs):
        return i * self.per + max((d + 1) * self.per + self.index[n] + 1 for n, d in needs)

    def one(self, name):
        assert self.names[self.made % self.per] == name, (name, self.names[self.made % self.per])
        self.made += 1
        return 1


def product3(nc, out, w, x, first, last):
    nc.tensor.matmul(out, w[0], x[0], start=first, stop=False)
    nc.tensor.matmul(out, w[0], x[1], start=False, stop=False)
    return nc.tensor.matmul(out, w[1], x[0], start=False, stop=last)


def load_ln_exp(nc, act):
    act.add_instruction(mybir.InstLoadActFuncSet(name=nc.get_next_instruction_name(), act_func_set_id=6,
                                                 engine=mybir.EngineType.Activation))


def gla_layer(nc, ctx, sb, sem, psum, keep, dram):
    st = ExitStack()
    with st:
        def tb(name, shape, dt=F32):
            return st.enter_context(nc.sbuf_tensor(name, shape, dt))

        def gsem(name):
            return sem("gla_" + name)

        W = BT // 2
        NC2 = NCH // 2
        WC = 2 * 768 + 2 * D + 2 * 1536 + 6 * D
        O_WO, O_GU = 1536, 1536 + 512
        O_WD = O_GU + 3072
        w_hi, w_lo = tb("gw_hi", [P, WC], F32R), tb("gw_lo", [P, WC], F32R)
        w_in = tb("gw_in", [P, WC])
        w_low = tb("gw_low", [P, DC, 16])
        w_up = tb("gw_up", [16, P])
        cols = tb("gcols", [P, 8])
        ones = tb("gones", [P, P])
        hblk = tb("ghblk", [P, P])
        tri = tb("gtri", [P, 64])
        hmask = tb("ghmask", [P, 8])
        bmask = tb("gbmask", [P, 8, 32])
        notfirst = tb("gnotfirst", [P, W])
        ident = keep["ident"]

        def two(name, shape, dt=F32):
            return [tb(f"g_{name}{h}", shape, dt) for h in range(2)]

        x, xcsq, rs, xn, hh = (two(n, s) for n, s in (
            ("x", [P, DC, W]), ("xcsq", [P, 2, DC, W]), ("rs", [P, 2, W]), ("xn", [P, DC, W]), ("h", [P, DC, W])))
        xc, sq = ([t[:, k] for t in xcsq] for k in range(2))
        hhi, hlo = two("hhi", [P, DC, W], F32R), two("hlo", [P, DC, W], F32R)
        sg, v = two("sg", [P, DC, W]), two("v", [P, 2, D])
        lb, cum, qe, ke, eb = (two(n, [P, W]) for n in ("lb", "cum", "qe", "ke", "eb"))
        kdT = two("kdT", [P, 2, P])
        a_hi, a_lo = ([two(f"a{n}{k}", [P, W], F32R) for k in range(2)] for n in ("hi", "lo"))
        af = [two(f"af{k}", [P, W]) for k in range(2)]
        S = two("S", [P, NC2 + 1, D])
        low, la = [af[0][h][0:16, :] for h in range(2)], af[1]
        qbd = [w_in[:, 2048 * h:2048 * h + 2048].rearrange("p (c h i) -> p c h i", c=NC2, h=8) for h in range(2)]
        atm = [w_in[:, 4096 + 1024 * h:5120 + 1024 * h].rearrange("p (a h i) -> p a h i", a=2, h=8) for h in range(2)]
        dsm = [t.rearrange("p a c n -> p (a c n)").rearrange("p (r a n) -> p r a n", r=2, a=2) for t in xcsq]

        s_win, s_small = [gsem(f"weights_loaded{k}") for k in range(2)], gsem("small_weights_loaded")
        s_x, s_x1 = [gsem(f"x_loaded{h}") for h in range(2)], [gsem(f"x1_stored{h}") for h in range(2)]
        s_const = gsem("constants")
        s_whi, s_wlo = gsem("weights_hi"), gsem("weights_lo")
        pe_s, act_s, dve_s = gsem("tensor_steps"), gsem("scalar_steps"), gsem("vector_steps")
        PARTS = ((0, O_WO), (O_WO, WC))
        CONSTS = 28

        front = {
            "pe": {"in_mean": 0, "in_var": 4.7, "low": 9.6, "q": 10.6, "k": 11.2, "z": 11.9, "gate": 14.9, "v": 16.1,
                   "kdT": 20.3, "dS": 21.8, "A0": 25.5, "A1": 26.3, "o": 30.9, "osum": 35.4, "wo": 42.9},
            "act": {"in_sq": 3.9, "in_ln1": 5.9, "in_ln2": 6.2, "in_rs": 6.6, "in_hi": 8.9, "low": 10.7, "abs": 12.9,
                   "e": 16.1, "ln": 16.4, "v": 17.7, "eb": 18.2, "enb": 18.5, "edk": 18.8, "silu": 20.4, "kdT": 21.2,
                   "osq0": 34, "osq1": 34.2, "lno": 37.4, "ro": 38, "oghi": 40.5},
            "dve": {"in_xc": 2.2, "in_h0": 7.5, "in_h1": 7.9, "in_lo": 9.7, "in_xn": 13.5, "zmin": 15.4, "graw": 17,
                   "cum": 17.4, "dcum": 18.1, "qe": 18.8, "ke": 19.1, "kd": 19.5, "qbd0": 19.8, "qbd1": 20.4, "qbd2":
                   21, "qbd3": 22, "dsm0": 23.8, "dsm1": 24.8, "S0": 25.4, "S1": 25.9, "S2": 26.7, "S3": 27.9, "atm0":
                   28.3, "atm1": 29.7, "og0": 38.8, "og1": 39.2, "og": 39.6, "oglo": 41.3, "xa": 45.8}}
        back = {
            "pe": {"rms2": 2, "gu0": 7, "gu1": 8.3, "down0": 12.3, "gu2": 12.9, "down1": 14.2, "down2": 18.4, "gu3":
                   19, "gu4": 20.5, "down3": 23.5, "gu5": 24.2, "down4": 27.2, "down5": 28.2, "out_mean": 30,
                   "out_var": 33.7, "next_mean": 38.4, "next_var": 42.1},
            "act": {"sq2": 1.2, "ln2": 3.2, "r2": 3.6, "h2hi": 5.3, "silu0": 8.6, "acthi0": 11, "silu1": 11.3, "acthi1":
                   12.6, "silu2": 14.5, "acthi2": 16.7, "silu3": 20.9, "acthi3": 22.3, "silu4": 22.6, "acthi4": 23.8,
                   "silu5": 25.8, "acthi5": 27, "out_sq": 32.1, "out_ln": 35.8, "out_rs": 36.2, "next_sq": 41.3,
                   "next_ln1": 43.2, "next_ln2": 43.6, "next_rs": 44, "next_hi": 45.9},
            "dve": {"h20": 4.2, "h21": 4.6, "h2lo": 6.1, "act0": 10.3, "actlo0": 11.6, "act1": 11.9, "actlo1": 13.2,
                   "act2": 15.1, "actlo2": 17.8, "act3": 21.6, "actlo3": 22.9, "act4": 23.2, "actlo4": 24.4, "act5":
                   26.3, "actlo5": 27.6, "xb": 29.1, "carry": 30.3, "out_xc": 31.2, "out_xn": 36.8, "x1": 37.5,
                   "next_xc": 40.4, "next_h0": 44.8, "next_h1": 45.2, "next_y": 46.4, "next_lo": 47}}
        shift, plan = {}, {}
        for e in ("pe", "act", "dve"):
            for n in front[e]:
                shift[e, n, 0] = shift[e, n, 1] = 0
            for n in back[e]:
                shift[e, n, 0], shift[e, n, 1] = 0, -1
            slots = [[(t, n, h) for n, t in front[e].items()] + [(t, n, 1 - h) for n, t in back[e].items()] for h in range(2)]
            plan[e] = [(n, h) for slot in slots for _, n, h in sorted(slot)]
        PE, AC, DV = Steps(plan["pe"]), Steps(plan["act"]), Steps(plan["dve"])
        ENG = {id(PE): "pe", id(AC): "act", id(DV): "dve"}

        def at(steps, names, of):
            e, n, h, i = of
            names = (names,) if isinstance(names, str) else names
            return steps.latest(i, [((m, h), shift[e, n, h] - shift[ENG[id(steps)], m, h]) for m in names])

        def block_of(of):
            e, n, h, i = of
            return i + shift[e, n, h]

        def later(of):
            return not (isinstance(of[3], int) and block_of(of) == 0)

        def columns(of):
            e, n, h, i = of
            return bass.ds(i * BT + (shift[e, n, h] * BT + h * W), W)

        def run(eng, s, e, steps, i, work):
            skipped = 0
            for k, (n, h) in enumerate(plan[e]):
                if isinstance(i, int) and not 0 <= i + shift[e, n, h] < NB:
                    skipped += 1
                    steps.one((n, h))
                    continue
                if skipped:
                    eng.wait_ge(s, k - skipped + (i + 1) * steps.per)
                    eng.sem_inc(s, skipped)
                    skipped = 0
                work(n, h, (e, n, h, i)).then_inc(s, steps.one((n, h)))

        def everywhere(eng, s, e, steps, work):
            eng.sem_inc(s, steps.per)
            run(eng, s, e, steps, 0, work)
            with eng.Fori(1, NB) as i:
                run(eng, s, e, steps, i, work)
            run(eng, s, e, steps, NB, work)

        def bank(h, k):
            return psum[:, 4 * h + k, :]

        def lower(h, k):
            return psum[:, 4 * h + k, 0:W]

        def upper(h, k):
            return psum[:, 4 * h + k, W:2 * W]

        def whl(off, n):
            return w_hi[:, off:off + n], w_lo[:, off:off + n]

        def bc2(ap):
            return ap.unsqueeze(1).broadcast_to([P, DC, W])

        def halves(ap):
            return ap.rearrange("p (a n) -> p a n", a=2)

        def o_view(h, half):
            return psum[:, 4 * h:4 * h + 4:3, half * P:half * P + P].rearrange("p r (a t) -> p r a t", a=2)

        block = st.enter_context(nc.Block())

        @block.sync
        def _(sp):
            def load_x(h, blk):
                sp.dma_start(x[h][:], dram["xT"][:, :, bass.ds(blk * BT + h * W, W)]).then_inc(s_x[h], 16)

            load_x(0, 0)
            sp.dma_start(cols[:], dram["cols"]).then_inc(s_small, 16)
            qkvg = w_in[:, 0:O_WO].rearrange("p (c n) -> p c n", c=2)
            at_col = 0
            for name, n in (("wq", 128), ("wk", 128), ("wv", 256), ("wg", 256)):
                sp.dma_start(qkvg[:, :, at_col:at_col + n], dram[name].rearrange("(c p) n -> p c n", p=P))\
                    .then_inc(s_win[0], 16)
                at_col += n
            sp.dma_start(w_low[:], dram["gk_w1"].rearrange("(c p) n -> p c n", p=P)).then_inc(s_small, 16)
            sp.dma_start(w_up[:], dram["gk_w2"]).then_inc(s_small, 16)
            load_x(1, 0)
            sp.dma_start(w_in[:, O_WO:O_GU].rearrange("p (c n) -> p c n", c=2),
                         dram["wo"].rearrange("(c p) n -> p c n", p=P)).then_inc(s_win[1], 16)
            sp.wait_ge(s_const, 3)
            gu = w_in[:, O_GU:O_WD].rearrange("p (c g n) -> p c g n", c=2, g=2)
            for g, name in enumerate(("w_gate", "w_up")):
                sp.dma_start(gu[:, :, g, 0:704], dram[name].rearrange("(c p) n -> p c n", p=P)).then_inc(s_win[1], 16)
            wd = w_in[:, O_WD:WC].rearrange("p (c n) -> p c n", c=6)
            sp.dma_start(wd[:, 0:5, :], dram["w_down"][0:640, :].rearrange("(c p) n -> p c n", p=P)).then_inc(s_win[1], 16)
            sp.dma_start(wd[0:64, 5, :], dram["w_down"][640:704, :]).then_inc(s_win[1], 16)

            def store_x1(h, i, shift_x1):
                sp.wait_ge(dve_s, DV.at(("x1", h), i - shift_x1))
                sp.dma_start(dram["x1"][:, :, bass.ds(i * BT + h * W, W)], hh[h][:]).then_inc(s_x1[h], 16)

            with sp.Fori(0, NB - 1) as i:
                for h in range(2):
                    store_x1(h, i, shift["dve", "x1", h])
                    load_x(h, i + 1)
            for h in range(2):
                store_x1(h, NB - 1, shift["dve", "x1", h])
            for h in range(2):
                sp.wait_ge(s_x1[h], 16 * NB)

        @block.gpsimd
        def _(pool):
            step = [0]

            def made(ins):
                step[0] += 1
                ins.then_inc(s_const, 1)
                pool.wait_ge(s_const, step[0])

            made(nc.gpsimd.memset(ones[:], 1.0 / D))
            made(nc.gpsimd.memset(w_in[:, O_GU:O_WD].rearrange("p (a n) -> p a n", a=4)[:, :, 704:768], 0.0))
            made(nc.gpsimd.memset(w_in[:, O_WD + 5 * D:WC], 0.0))
            made(nc.gpsimd.memset(keep["eps"][:, 0:1], EPS_LN))
            made(nc.gpsimd.memset(keep["eps"][:, 1:2], EPS_RMS))
            made(nc.gpsimd.memset(keep["eps"][:, 2:3], EPS_LN * EPS_RMS))
            for h in range(2):
                made(nc.gpsimd.memset(S[h][:], 0.0))
            made(nc.gpsimd.memset(notfirst[:], 1.0))
            made(nc.gpsimd.memset(notfirst[:].rearrange("p (c t) -> p c t", c=NC2)[:, :, 0:1], 0.0))
            made(nc.gpsimd.memset(hmask[:], 1.0))
            made(nc.gpsimd.affine_select(out=hmask[:], in_=hmask[:], compare_op=ALU.is_ge, fill=0.0, base=0,
                                         pattern=[[-16, 8]], channel_multiplier=1))
            made(nc.gpsimd.affine_select(out=hmask[:], in_=hmask[:], compare_op=ALU.is_ge, fill=0.0, base=15,
                                         pattern=[[16, 8]], channel_multiplier=-1))
            made(nc.gpsimd.memset(bmask[:], 1.0))
            made(nc.gpsimd.affine_select(out=bmask[:], in_=bmask[:], compare_op=ALU.is_ge, fill=0.0, base=0,
                                         pattern=[[-16, 8], [0, 32]], channel_multiplier=1))
            made(nc.gpsimd.affine_select(out=bmask[:], in_=bmask[:], compare_op=ALU.is_ge, fill=0.0, base=15,
                                         pattern=[[16, 8], [0, 32]], channel_multiplier=-1))
            made(nc.gpsimd.memset(ident[:], 0.0))
            made(nc.gpsimd.affine_select(out=ident[:], in_=ident[:], compare_op=ALU.not_equal, fill=1.0, base=0,
                                         pattern=[[-1, P]], channel_multiplier=1))
            made(nc.gpsimd.memset(tri[:], 1.0))
            for r in range(2):
                t = tri[64 * r:64 * r + 64, :]
                made(nc.gpsimd.affine_select(out=t, in_=t, compare_op=ALU.is_ge, fill=0.0, base=0,
                                             pattern=[[1, 64]], channel_multiplier=-1))
            made(nc.gpsimd.memset(hblk[:], 0.0))
            for g in range(4):
                made(nc.gpsimd.memset(hblk[32 * g:32 * g + 32, 32 * g:32 * g + 32], 1.0 / 32))
            made(nc.gpsimd.memset(keep["cmask"][:], 0.0))
            made(nc.gpsimd.affine_select(out=keep["cmask"][:], in_=keep["cmask"][:], compare_op=ALU.is_ge,
                                         fill=MASKED, base=0, pattern=[[-1, P]], channel_multiplier=1))
            assert step[0] == CONSTS, step[0]

        @block.tensor
        def _(pe):
            def stat(out, src):
                nc.tensor.matmul(out, ones[:], src[:, 0, :], start=True, stop=False)
                return nc.tensor.matmul(out, ones[:], src[:, 1, :], start=False, stop=True)

            def proj(out, h, offset, step):
                for c in range(DC):
                    last = product3(nc, out, whl(offset + c * step, P), (hhi[h][:, c, :], hlo[h][:, c, :]), c == 0, c == 1)
                return last

            def work(n, h, of):
                if n == "in_mean":
                    pe.wait_ge(s_x[h], (block_of(of) + 1) * 16)
                    if later(of):
                        pe.wait_ge(dve_s, DV.at(("x1", h), block_of(of) - 1 - shift["dve", "x1", h]))
                    return stat(lower(h, 3), x[h])
                if n == "in_var":
                    pe.wait_ge(act_s, at(AC, "in_sq", of))
                    return stat(lower(h, 2), sq[h])
                if n == "low":
                    pe.wait_ge(s_small, 3 * 16)
                    pe.wait_ge(dve_s, at(DV, "in_h1", of))
                    for c in range(DC):
                        last = nc.tensor.matmul(psum[0:16, 4 * h + 2, 0:W], w_low[:, c, :], hh[h][:, c, :],
                                                start=c == 0, stop=c == 1)
                    return last
                if n == "q":
                    pe.wait_ge(s_wlo, 1)
                    pe.wait_ge(dve_s, at(DV, "in_lo", of))
                    return proj(lower(h, 0), h, 0, 768)
                if n == "k":
                    return proj(upper(h, 0), h, 128, 768)
                if n == "z":
                    pe.wait_ge(act_s, at(AC, "low", of))
                    return nc.tensor.matmul(upper(h, 2), w_up[:], low[h], start=True, stop=True)
                if n == "gate":
                    proj(lower(h, 1), h, 512, 768)
                    return proj(upper(h, 1), h, 640, 768)
                if n == "v":
                    for t in range(2):
                        for c in range(DC):
                            last = product3(nc, psum[:, 4 * h + 3, t * D:t * D + D],
                                            (hhi[h][:, c, t * P:(t + 1) * P], hlo[h][:, c, t * P:(t + 1) * P]),
                                            whl(c * 768 + 256, D), c == 0, c == 1)
                    return last
                if n == "kdT":
                    pe.wait_ge(dve_s, at(DV, "kd", of))
                    for t in range(2):
                        last = nc.tensor.transpose(psum[:, 4 * h + 2, t * P:(t + 1) * P], lb[h][:, t * P:(t + 1) * P],
                                                   ident[:])
                    return last
                if n == "dS":
                    pe.wait_ge(act_s, at(AC, ("kdT", "v"), of))
                    for r in range(2):
                        for p in range(2):
                            last = nc.tensor.matmul(psum[:, 4 * h + 3 * r, p * D:p * D + D],
                                                    kdT[h][64 * r:64 * r + 64, p, :], v[h][64 * r:64 * r + 64, p, :],
                                                    start=True, stop=True)
                    return last
                if n in ("A0", "A1"):
                    p = int(n[1])
                    pe.wait_ge(dve_s, at(DV, f"qbd{2 * p + 1}", of))
                    pe.wait_ge(act_s, at(AC, ("silu", "kdT")[p], of))
                    for r in range(2):
                        c = 2 * p + r
                        last = nc.tensor.matmul(psum[64 * r:64 * r + 64, 4 * h + 1 + p, :], ke[h][:, c * 64:c * 64 + 64],
                                                qbd[h][:, c], start=True, stop=True)
                    return last
                if n == "o":
                    pe.wait_ge(dve_s, at(DV, ("atm1", f"S{NC2 - 1}"), of))
                    for c in range(NC2):
                        p, r = c // 2, c % 2
                        for half in range(2):
                            a = half * P + p * 64
                            nc.tensor.matmul(psum[:, 4 * h + 3 * r, a:a + 64], S[h][:, c, half * P:half * P + P],
                                             qe[h][:, c * 64:c * 64 + 64], start=True, stop=False, skip_group_check=True)
                            for g in range(4):
                                hd = 4 * half + g
                                last = nc.tensor.matmul(psum[32 * g:32 * g + 32, 4 * h + 3 * r, a:a + 64],
                                                        v[h][64 * r:64 * r + 64, p, hd * 32:hd * 32 + 32],
                                                        atm[h][64 * r:64 * r + 64, p, hd, :], start=False, stop=True,
                                                        skip_group_check=True)
                    return last
                if n == "osum":
                    pe.wait_ge(act_s, at(AC, "osq1", of))
                    for half in range(2):
                        last = nc.tensor.matmul(psum[:, 4 * h + 1, half * W:half * W + W], hblk[:], sq[h][:, half, :],
                                                start=True, stop=True)
                    return last
                if n == "wo":
                    pe.wait_ge(s_wlo, 2)
                    pe.wait_ge(dve_s, at(DV, "oglo", of))
                    proj(lower(h, 2), h, O_WO, D)
                    return proj(upper(h, 2), h, O_WO + P, D)
                if n == "rms2":
                    pe.wait_ge(act_s, at(AC, "sq2", of))
                    return stat(lower(h, 0), sq[h])
                if n[:2] == "gu":
                    j = int(n[2:])
                    pe.wait_ge(dve_s, at(DV, "h2lo" if j < 2 else f"act{j - 2}", of))
                    proj(lower(h, j % 2), h, O_GU + j * P, 1536)
                    return proj(upper(h, j % 2), h, O_GU + 768 + j * P, 1536)
                if n[:4] == "down":
                    j = int(n[4:])
                    pe.wait_ge(dve_s, at(DV, f"actlo{j}", of))
                    for m in range(2):
                        last = product3(nc, lower(h, 2 + m), whl(O_WD + j * D + m * P, P),
                                        (a_hi[j % 2][h][:], a_lo[j % 2][h][:]), j == 0, j == 5)
                    return last
                if n == "out_mean":
                    pe.wait_ge(dve_s, at(DV, "xb", of))
                    return stat(lower(h, 0), xn[h])
                if n == "next_mean":
                    pe.wait_ge(dve_s, at(DV, "x1", of))
                    return stat(lower(h, 0), hh[h])
                assert n in ("out_var", "next_var")
                pe.wait_ge(act_s, at(AC, n[:-3] + "sq", of))
                return stat(lower(h, 1), sq[h])

            pe.wait_ge(s_const, CONSTS)
            everywhere(pe, pe_s, "pe", PE, work)

        @block.scalar
        def _(act):
            loaded = [None]

            def ln_exp():
                if loaded[0] != "ln_exp":
                    load_ln_exp(nc, act)
                loaded[0] = "ln_exp"

            LN = {"in_ln1": (0, 2, 0), "in_ln2": (1, 2, 2), "next_ln1": (0, 1, 0), "next_ln2": (1, 1, 2),
                  "out_ln": (0, 1, 0), "ln2": (1, 0, 1)}
            LN_EXP = ("in_rs", "next_rs", "out_rs", "r2", "e", "ln", "eb", "enb", "edk", "lno", "ro")
            SPLITS = {"in_hi": (0,), "low": (1,)}

            def work(n, h, of):
                if h == 0 and not later(of) and n in SPLITS:
                    for k in SPLITS[n]:
                        a, z = PARTS[k]
                        act.wait_ge(s_win[k], (4, 5)[k] * 16)
                        act.wait_ge(s_const, 3)
                        nc.scalar.activation(w_hi[:, a:z], w_in[:, a:z], ACT.Copy).then_inc(s_whi, 1)
                if n in LN or n in LN_EXP:
                    ln_exp()
                if n in ("in_sq", "out_sq", "next_sq"):
                    act.wait_ge(dve_s, at(DV, n[:-2] + "xc", of))
                    return nc.scalar.activation(sq[h], xc[h], ACT.Square)
                if n in LN:
                    k, b, e = LN[n]
                    act.wait_ge(pe_s, at(PE, "rms2" if n == "ln2" else n.split("_")[0] + "_var", of))
                    return nc.scalar.activation(rs[h][:, k, :], lower(h, b), ACT.Ln, bias=keep["eps"][:, e:e + 1],
                                                scale=1.0 + EPS_RMS if e == 2 else 1.0)
                if n in ("in_rs", "next_rs"):
                    act.wait_ge(act_s, at(AC, n[:-2] + "ln2", of))
                    return nc.scalar.activation(rs[h][:], rs[h][:], ACT.Exp, scale=-0.5)
                if n in ("out_rs", "r2"):
                    k = int(n == "r2")
                    act.wait_ge(act_s, at(AC, "ln2" if k else "out_ln", of))
                    return nc.scalar.activation(rs[h][:, k, :], rs[h][:, k, :], ACT.Exp, scale=-0.5)
                if n in ("in_hi", "h2hi", "oghi"):
                    act.wait_ge(dve_s, at(DV, {"in_hi": "in_h1", "h2hi": "h21", "oghi": "og"}[n], of))
                    return nc.scalar.activation(hhi[h][:], hh[h][:], ACT.Copy)
                if n == "silu":
                    act.wait_ge(pe_s, at(PE, "gate", of))
                    loaded[0] = "silu"
                    return nc.scalar.activation(sg[h][:].rearrange("p a n -> p (a n)"), bank(h, 1), ACT.Silu)
                if n == "low":
                    act.wait_ge(pe_s, at(PE, "low", of))
                    return nc.scalar.activation(low[h], psum[0:16, 4 * h + 2, 0:W], ACT.Copy)
                if n == "v":
                    act.wait_ge(pe_s, at(PE, "v", of))
                    return nc.scalar.activation(v[h][:].rearrange("p t n -> p (t n)"), bank(h, 3), ACT.Copy)
                if n == "abs":
                    act.wait_ge(pe_s, at(PE, "z", of))
                    return nc.scalar.activation(la[h][:], upper(h, 2), ACT.Abs, bias=cols[:, 6:7])
                if n == "e":
                    act.wait_ge(act_s, at(AC, "abs", of))
                    return nc.scalar.activation(la[h][:], la[h][:], ACT.Exp, scale=-1.0)
                if n == "ln":
                    act.wait_ge(act_s, at(AC, "e", of))
                    return nc.scalar.activation(la[h][:], la[h][:], ACT.Ln, bias=1.0)
                if n in ("eb", "enb", "edk"):
                    act.wait_ge(dve_s, at(DV, "dcum" if n == "edk" else "cum", of))
                    out, in_ = {"eb": (eb, cum), "enb": (ke, cum), "edk": (lb, lb)}[n]
                    return nc.scalar.activation(out[h][:], in_[h][:], ACT.Exp, scale=(-1.0 if n == "enb" else 1.0) / 16)
                if n == "kdT":
                    act.wait_ge(pe_s, at(PE, "kdT", of))
                    return nc.scalar.activation(kdT[h][:].rearrange("p t n -> p (t n)"), lower(h, 2), ACT.Copy)
                if n in ("osq0", "osq1"):
                    half = int(n[3])
                    act.wait_ge(pe_s, at(PE, "o", of))
                    return nc.scalar.activation(sq[h][:, half, :].rearrange("p (a r t) -> p r a t", a=2, r=2),
                                                o_view(h, half), ACT.Square)
                if n == "lno":
                    act.wait_ge(pe_s, at(PE, "osum", of))
                    return nc.scalar.activation(rs[h][:], halves(bank(h, 1)), ACT.Ln, bias=keep["eps"][:, 1:2])
                if n == "ro":
                    act.wait_ge(act_s, at(AC, "lno", of))
                    return nc.scalar.activation(rs[h][:], rs[h][:], ACT.Exp, scale=-0.5)
                if n == "sq2":
                    act.wait_ge(dve_s, at(DV, "xa", of))
                    return nc.scalar.activation(sq[h], xn[h][:], ACT.Square)
                if n[:4] == "silu":
                    j = int(n[4:])
                    act.wait_ge(pe_s, at(PE, f"gu{j}", of))
                    loaded[0] = "silu"
                    return nc.scalar.activation(sg[h][:, j % 2, :], lower(h, j % 2), ACT.Silu)
                if n[:5] == "acthi":
                    j = int(n[5:])
                    act.wait_ge(dve_s, at(DV, f"act{j}", of))
                    if j >= 2:
                        act.wait_ge(pe_s, at(PE, f"down{j - 2}", of))
                    return nc.scalar.activation(a_hi[j % 2][h][:], af[j % 2][h][:], ACT.Copy)
                assert n == "next_hi"
                act.wait_ge(dve_s, at(DV, "next_h1", of))
                return nc.scalar.activation(keep["xx_hi"][:, :, columns(of)], sq[h], ACT.Copy)

            act.wait_ge(s_const, CONSTS)
            act.sem_inc(act_s, AC.per)
            loaded[0] = None
            run(act, act_s, "act", AC, 0, work)
            loaded[0] = None
            with act.Fori(1, NB) as i:
                run(act, act_s, "act", AC, i, work)
            loaded[0] = None
            run(act, act_s, "act", AC, NB, work)

        @block.vector
        def _(dve):
            def tt(out, a, b, op):
                return nc.vector.tensor_tensor(out, a, b, op)

            def stt(out, a, s, b, op0=ALU.mult, op1=ALU.mult):
                return nc.vector.scalar_tensor_tensor(out=out, in0=a, scalar=s, in1=b, op0=op0, op1=op1)

            def split_weights(k):
                a, z = PARTS[k]
                dve.wait_ge(s_whi, k + 1)
                tt(w_lo[:, a:z], w_in[:, a:z], w_hi[:, a:z].bitcast(F32), ALU.subtract).then_inc(s_wlo, 1)

            def work(n, h, of):
                if h == 0 and not later(of) and n in ("in_lo", "in_xn"):
                    split_weights(int(n == "in_xn"))
                if n in ("in_xc", "out_xc", "next_xc"):
                    kind = n[:-3]
                    dve.wait_ge(pe_s, at(PE, kind + "_mean", of))
                    if kind == "in" and later(of):
                        dve.wait_ge(dve_s, DV.at(("next_lo", h), block_of(of) - 1 - shift["dve", "next_lo", h]))
                    src = {"in": x, "out": xn, "next": hh}[kind][h]
                    return tt(xc[h], src[:], bc2(lower(h, 3 if kind == "in" else 0)), ALU.subtract)
                if n in ("in_h0", "in_h1", "next_h0", "next_h1"):
                    kind, c = n[:-3], int(n[-1])
                    dve.wait_ge(act_s, at(AC, kind + "_rs", of))
                    if kind == "in":
                        dve.wait_ge(s_small, 3 * 16)
                    out, col = (hh[h], 0) if kind == "in" else (sq[h], 4)
                    return stt(out[:, c, :], xc[h][:, c, :], cols[:, col + c:col + c + 1], rs[h][:, 1, :])
                if n in ("in_xn", "out_xn"):
                    if n == "out_xn":
                        dve.wait_ge(act_s, at(AC, "out_rs", of))
                    return tt(xn[h][:], xc[h], bc2(rs[h][:, 0, :]), ALU.mult)
                if n == "next_y":
                    return tt(keep["y"][:, :, columns(of)], xc[h], bc2(rs[h][:, 0, :]), ALU.mult)
                if n in ("in_lo", "oglo", "h2lo"):
                    dve.wait_ge(act_s, at(AC, {"in_lo": "in_hi", "oglo": "oghi", "h2lo": "h2hi"}[n], of))
                    return tt(hlo[h][:], hh[h][:], hhi[h][:].bitcast(F32), ALU.subtract)
                if n == "zmin":
                    dve.wait_ge(act_s, at(AC, "abs", of))
                    return nc.vector.tensor_scalar(lb[h][:], upper(h, 2), cols[:, 6:7], 0.0, ALU.add, ALU.min)
                if n == "graw":
                    dve.wait_ge(act_s, at(AC, "ln", of))
                    dve.wait_ge(dve_s, at(DV, "zmin", of))
                    return tt(lb[h][:], lb[h][:], la[h][:], ALU.subtract)
                if n == "cum":
                    dve.wait_ge(dve_s, at(DV, "graw", of))
                    return nc.vector.tensor_tensor_scan(cum[h][:], notfirst[:], lb[h][:], 0.0, ALU.mult, ALU.add)
                if n == "dcum":
                    dve.wait_ge(dve_s, at(DV, "cum", of))
                    cum3 = cum[h][:].rearrange("p (c t) -> p c t", c=NC2)
                    return tt(lb[h][:].rearrange("p (c t) -> p c t", c=NC2),
                              cum3[:, :, 63:64].broadcast_to([P, NC2, 64]), cum3, ALU.subtract)
                if n == "qe":
                    dve.wait_ge(act_s, at(AC, "eb", of))
                    return stt(qe[h][:], lower(h, 0), 16 ** -0.5, eb[h][:])
                if n == "ke":
                    dve.wait_ge(act_s, at(AC, "enb", of))
                    return tt(ke[h][:], upper(h, 0), ke[h][:], ALU.mult)
                if n == "kd":
                    dve.wait_ge(act_s, at(AC, "edk", of))
                    return tt(lb[h][:], upper(h, 0), lb[h][:], ALU.mult)
                if n[:3] == "qbd":
                    c = int(n[3:])
                    dve.wait_ge(dve_s, at(DV, "qe", of))
                    return tt(qbd[h][:, c], qe[h][:, c * 64:c * 64 + 64].unsqueeze(1).broadcast_to([P, 8, 64]),
                              hmask[:].unsqueeze(2).broadcast_to([P, 8, 64]), ALU.mult)
                if n in ("dsm0", "dsm1"):
                    r = int(n[3])
                    dve.wait_ge(pe_s, at(PE, "dS", of))
                    bm = bmask[:].rearrange("p a b -> p (a b)").unsqueeze(1).broadcast_to([P, 2, D])
                    return tt(dsm[h][:, r], halves(bank(h, 3 * r)), bm, ALU.mult)
                if n[0] == "S":
                    c = int(n[1:])
                    dve.wait_ge(dve_s, at(DV, f"S{c - 1}" if c else "dsm1", of))
                    return stt(S[h][:, c + 1, :], S[h][:, c, :], eb[h][:, c * 64 + 63:c * 64 + 64],
                               dsm[h][:, c % 2, c // 2, :], ALU.mult, ALU.add)
                if n in ("atm0", "atm1"):
                    p = int(n[3])
                    dve.wait_ge(pe_s, at(PE, f"A{p}", of))
                    return tt(atm[h][:, p], bank(h, 1 + p).rearrange("p (h i) -> p h i", h=8),
                              tri[:].unsqueeze(1).broadcast_to([P, 8, 64]), ALU.mult)
                if n in ("og0", "og1"):
                    half = int(n[2])
                    dve.wait_ge(act_s, at(AC, "ro", of))
                    return tt(hh[h][:, half, :].rearrange("p (a r t) -> p r a t", a=2, r=2), o_view(h, half),
                              rs[h][:, half, :].rearrange("p (a r t) -> p r a t", a=2, r=2), ALU.mult)
                if n == "og":
                    dve.wait_ge(dve_s, at(DV, "og1", of))
                    return stt(hh[h][:], hh[h][:], cols[:, 7:8], sg[h][:])
                if n == "xa":
                    dve.wait_ge(pe_s, at(PE, "wo", of))
                    return tt(xn[h][:], xn[h][:], halves(bank(h, 2)), ALU.add)
                if n in ("h20", "h21"):
                    c = int(n[2])
                    dve.wait_ge(act_s, at(AC, "r2", of))
                    return stt(hh[h][:, c, :], xn[h][:, c, :], cols[:, 2 + c:3 + c], rs[h][:, 1, :])
                if n[:5] == "actlo":
                    j = int(n[5:])
                    dve.wait_ge(act_s, at(AC, f"acthi{j}", of))
                    return tt(a_lo[j % 2][h][:], af[j % 2][h][:], a_hi[j % 2][h][:].bitcast(F32), ALU.subtract)
                if n[:3] == "act":
                    j = int(n[3:])
                    dve.wait_ge(act_s, at(AC, f"silu{j}", of))
                    return tt(af[j % 2][h][:], sg[h][:, j % 2, :], upper(h, j % 2), ALU.mult)
                if n == "xb":
                    dve.wait_ge(pe_s, at(PE, "down5", of))
                    return tt(xn[h][:], xn[h][:], psum[:, 4 * h + 2:4 * h + 4, 0:W], ALU.add)
                if n == "carry":
                    return nc.vector.tensor_copy(S[h][:, 0, :], S[h][:, NC2, :])
                if n == "x1":
                    dve.wait_ge(dve_s, at(DV, "out_xn", of))
                    return tt(hh[h][:], xn[h][:], x[h][:], ALU.add)
                assert n == "next_lo"
                dve.wait_ge(act_s, at(AC, "next_hi", of))
                dve.wait_ge(s_x1[h], (block_of(of) + 1) * 16)
                return tt(keep["xx_lo"][:, :, columns(of)], sq[h], keep["xx_hi"][:, :, columns(of)].bitcast(F32),
                          ALU.subtract)

            dve.wait_ge(s_const, CONSTS)
            everywhere(dve, dve_s, "dve", DV, work)


def attention_layer(nc, ctx, sb, sem, psum, keep, dram):
    SCALE = float(QHD) ** -0.5
    HP = HEADS // 2
    st = ExitStack()
    with st:
        def tb(name, shape, dt=F32):
            return st.enter_context(nc.sbuf_tensor(name, shape, dt))

        def asem(name):
            return sem("attn_" + name)

        KINDS = "qkvo"
        w_in = tb("aw_in", [P, 2, 256])
        w_hi = {k: tb(f"aw_{k}hi", [P, 2, 256], F32R) for k in KINDS}
        w_lo = {k: tb(f"aw_{k}lo", [P, 2, 256], F32R) for k in KINDS}
        qk_hi = [tb(f"a_qkhi{u}", [P, 2, 1024], F32R) for u in range(2)]
        qk_lo = [tb(f"a_qklo{u}", [P, 2, 1024], F32R) for u in range(2)]
        v_hi = [tb(f"a_vhi{b}", [P, 8, 256], F32R) for b in range(2)]
        v_lo = [tb(f"a_vlo{b}", [P, 8, 256], F32R) for b in range(2)]
        prob0, prob = tb("a_probfirst", [P, P]), [tb(f"a_prob{k}", [P, 1024]) for k in range(3)]
        pt_hi = [tb(f"a_pthi{g}", [P, 4 + 4 * g, 512], F32R) for g in range(2)]
        pt_lo = [tb(f"a_ptlo{g}", [P, 4 + 4 * g, 512], F32R) for g in range(2)]
        o_hi = [tb(f"a_ohi{h}", [P, 2, 512], F32R) for h in range(2)]
        o_lo = [tb(f"a_olo{h}", [P, 2, 512], F32R) for h in range(2)]
        nmx, tot, inv = (tb(f"a_{n}", [P, 8]) for n in ("nmx", "tot", "inv"))
        S = [psum[:, 0:2, :].rearrange("p a n -> p (a n)"), psum[:, 2:4, :].rearrange("p a n -> p (a n)")]
        T = [psum[:, 4, :], psum[:, 5, :]]
        O = psum[:, 6, :]
        J = psum[:, 7, :]
        ident = keep["ident"]
        xx = (keep["xx_hi"], keep["xx_lo"])

        def xcols(k, c, b, g):
            return xx[k][:, c, :].rearrange("p (j b t) -> p j b t", j=4, b=2)[:, 2 * g:2 * g + 2, b, :]

        def xtile(k, c, b, t):
            at = (t // 2) * 512 + b * 256 + (t % 2) * P
            return xx[k][:, c, at:at + P]

        def loaded(k, first_pair):
            if first_pair and k in "qk":
                return prob["qk".index(k)][:, 0:512].rearrange("p (c n) -> p c n", c=2)
            return w_in[:]

        def probs(s):
            u, t = divmod(s, 8)
            return prob0 if t == 0 else prob[((0, 1, 2, 1)[u] + t - 1) % 3]

        def turn_parts(s):
            return 1 + (s % 8 >= 4)

        tb_index, n = {}, 0
        for s in range(32):
            for part in range(turn_parts(s)):
                tb_index[s, part] = n
                n += 1
        assert n % 2 == 0

        def at_step(s, later):
            return (s + later) % 32, (s + later) // 32

        QK_AT, REST_AT = (0, 1, 3, 4), (2, 5, 6, 7)
        SPLIT_AT = {8: ("o", 0), 16: ("v", 1), 21: ("q", 1), 23: ("k", 1)}
        POSITION = {
            "pe": {
                "bank_j": (0.05, 0.05, 0.05, 0.05, 0.05, 0.05, 0.05, 0.05),
                "score": (-0.6, -0.4, -0.85, -0.55, -0.75, -0.45, 0.1, -0.15),
                "turn": (0.55, 0.75, 0.15, 0.05, -0.35, -0.15, 0.75, 0.75),
                "pv": {2: -0.25, 6: -0.35}},
            "act": {
                "exp": (-1.3, -1.2, -1.5, -1.3, -1.5, -0.7, -0.1, -0.5),
                "turned": (-0.8, -0.4, -0.4, 1.05, 0.4, -0.25, 0.55, -0.35),
                "bank_j": (0.3, 0.3, 0.5, 1.2, 1.9, 1.15, 0.55, 0.15),
                "bank_o": {2: 0.4, 6: 0.8},
                "weights": {0: 0.4, 5: 0.9, 7: 0.1}},
            "dve": {
                "max": (-0.6, -1.1, -0.6, -1.5, -1, -0.9, -1, -0.1),
                "norm": (0.1, 0.6, -0.4, -1, -1, 0.1, 0.3, -0),
                "turned": (-0.15, 0.15, 0.8, 0.05, 0.5, -0.2, 0.45, 0.1),
                "bank_j": (0, 1.3, 0.45, 0.65, 0.95, 0.45, 0.75, 0.15),
                "bank_o": {2: 0.4, 6: 2.2},
                "weights": {0: 2, 5: 1.3, 7: 0.8}}}
        placed = {"pe": [], "act": [], "dve": []}

        def put(engine, kind, s, name, pairs_later):
            placed[engine].append((s + POSITION[engine][kind][s % 8], len(placed[engine]), name, pairs_later))

        for s in range(32):
            u, t = divmod(s, 8)
            if t in QK_AT:
                j_use, j_sh = ("qk", (u + 1) % 4, QK_AT.index(t)), int(u == 3)
            elif u % 2:
                j_use, j_sh = ("v", (u + 1) % 4 // 2, REST_AT.index(t)), int(u == 3)
            else:
                k = REST_AT.index(t)
                j_use, j_sh = ("oproj", (u // 2 - 1) % 2, k // 2, k % 2), -int(u == 0)
            pv = {6: ((u, 0), 0), 2: (((u - 1) % 4, 1), -int(u == 0))}.get(t)
            s2, sh2 = at_step(s, 2)
            s1, sh1 = at_step(s, 1)
            sm1, shm1 = at_step(s, -1)
            sm2, shm2 = at_step(s, -2)
            put("pe", "bank_j", s, j_use, j_sh)
            put("pe", "score", s, ("score", s2), sh2)
            for part in range(turn_parts(sm1)):
                put("pe", "turn", s, ("turn", sm1, part), shm1)
            put("act", "exp", s, ("exp", s), 0)
            for w in ("mask", "max"):
                put("dve", "max", s, (w, s1), sh1)
            for w in ("inv", "norm"):
                put("dve", "norm", s, (w, s), 0)
            for part in range(turn_parts(sm2)):
                put("act", "turned", s, ("turnhi", sm2, part), shm2)
                put("dve", "turned", s, ("turnlo", sm2, part), shm2)
            if j_use[0] == "oproj":
                put("dve", "bank_j", s, ("add",) + j_use[1:], j_sh)
            else:
                put("act", "bank_j", s, (j_use[0] + "hi",) + j_use[1:], j_sh)
                put("dve", "bank_j", s, (j_use[0] + "lo",) + j_use[1:], j_sh)
            if pv:
                put("pe", "pv", s, ("pv",) + pv[0], pv[1])
                put("act", "bank_o", s, ("ohi",) + pv[0], pv[1])
                put("dve", "bank_o", s, ("olo",) + pv[0], pv[1])
            if s in SPLIT_AT:
                put("act", "weights", s, ("w", SPLIT_AT[s][0], "hi"), SPLIT_AT[s][1])
                put("dve", "weights", s, ("w", SPLIT_AT[s][0], "lo"), SPLIT_AT[s][1])

        def in_order(steps):
            laps = [(x - x // 32 * 32, k, name, pairs_later - int(x // 32)) for x, k, name, pairs_later in steps]
            return [(name, pairs_later) for _, _, name, pairs_later in sorted(laps)]

        pe_plan, act_plan, dve_plan = (in_order(placed[e]) for e in ("pe", "act", "dve"))
        PE, AC, DV = (Steps([x for x, _ in p]) for p in (pe_plan, act_plan, dve_plan))
        shift = {**dict(pe_plan), **dict(act_plan), **dict(dve_plan)}
        pe_s, act_s, dve_s = asem("tensor_steps"), asem("scalar_steps"), asem("vector_steps")
        s_win = {k: asem(f"weights_{k}_loaded") for k in KINDS}
        s_zero, s_pad = asem("zeros"), asem("padding")

        def at(steps, name, i, of=None):
            return steps.at(name, i + (shift[of] - shift[name] if of else 0))

        def done_for(name, of):
            return name, shift[of] - shift[name]

        J_USERS = [x for x, _ in pe_plan if x[0] in ("qk", "v", "oproj")]

        STARTERS = [x for x, sh in pe_plan if x in J_USERS and sh == 1]

        def j_bank(name, i, pair_shift):
            first = isinstance(i, int) and i + pair_shift == 0 and name in STARTERS
            return O if first and STARTERS.index(name) % 2 else J

        def j_reader(name):
            if name[0] == "qk":
                return ("qklo",) + name[1:]
            if name[0] == "v":
                return ("vlo",) + name[1:]
            return ("add",) + name[1:]

        def run(eng, s, plan, steps, i, kind, work):
            lo, hi = {"before": (-1, -1), "first": (0, 0), "middle": (1, HP - 2), "last": (HP - 1, HP - 1),
                      "after": (HP, HP)}[kind]
            skipped = 0
            for k, (name, sh) in enumerate(plan):
                if lo + sh < 0 or hi + sh >= HP:
                    assert kind != "middle"
                    skipped += 1
                    steps.one(name)
                    continue
                if skipped:
                    if k - skipped + (i + 1) * steps.per:
                        eng.wait_ge(s, k - skipped + (i + 1) * steps.per)
                    eng.sem_inc(s, skipped)
                    skipped = 0
                work(name, i).then_inc(s, steps.one(name))
            if skipped and kind != "after":
                if k + 1 - skipped + (i + 1) * steps.per:
                    eng.wait_ge(s, k + 1 - skipped + (i + 1) * steps.per)
                eng.sem_inc(s, skipped)

        def everywhere(eng, s, plan, steps, work):
            run(eng, s, plan, steps, -1, "before", work)
            run(eng, s, plan, steps, 0, "first", work)
            with eng.Fori(1, HP - 1) as i:
                run(eng, s, plan, steps, i, "middle", work)
            run(eng, s, plan, steps, HP - 1, "last", work)
            run(eng, s, plan, steps, HP, "after", work)

        block = st.enter_context(nc.Block())

        @block.sync
        def _(sp):
            def load(k, pair, before):
                sp.wait_ge(*before)
                sp.dma_start(w_in[:], dram["aw_" + k][:, pair]).then_inc(s_win[k], 16)

            def split(k, i):
                return dve_s, DV.at(("w", k, "lo"), i)

            for k in "vqk":
                sp.dma_start(loaded(k, True), dram["aw_" + k][:, 0]).then_inc(s_win[k], 16)
            with sp.Fori(0, HP - 1) as i:
                load("o", i, split("k", i - 1))
                load("v", i + 1, split("o", i))
                load("q", i + 1, split("v", i))
                load("k", i + 1, split("q", i))
            load("o", HP - 1, split("k", HP - 2))

        @block.gpsimd
        def _(pool):
            nc.gpsimd.memset(prob0[:], 0.0).then_inc(s_zero, 1)

        @block.tensor
        def _(pe):
            def work(name, i):
                w = name[0]
                sh = shift[name]
                needs = []
                if w in ("qk", "v", "oproj"):
                    k = J_USERS.index(name)
                    out = j_bank(name, i, sh)
                    starter = isinstance(i, int) and i + sh == 0 and name in STARTERS
                    for back in range(2 if starter else 1, len(J_USERS)):
                        prev, turn = J_USERS[k - back], (i if k >= back else i - 1)
                        if not isinstance(i, int) or 0 <= turn + shift[prev] < HP:
                            needs.append((j_reader(prev), -int(k < back) + shift[prev] - shift[j_reader(prev)]))
                            break
                if w == "qk":
                    _, u, part = name
                    which, g, b, h = part % 2, part // 2, u // 2, u % 2
                    if part < 2:
                        needs.append(done_for(("w", "qk"[which], "lo"), name))
                    if needs:
                        pe.wait_ge(dve_s, DV.latest(i, needs))
                    for c in range(DC):
                        last = product3(nc, out, (w_hi["qk"[which]][:, c, h * P:h * P + P],
                                                w_lo["qk"[which]][:, c, h * P:h * P + P]),
                                        (xcols(0, c, b, g), xcols(1, c, b, g)), c == 0, c == 1)
                    return last
                if w == "v":
                    _, b, pair = name
                    if pair == 0:
                        needs.append(done_for(("w", "v", "lo"), name))
                    pe.wait_ge(dve_s, DV.latest(i, needs))
                    for t in range(2):
                        for c in range(DC):
                            last = product3(nc, out[:, t * 256:t * 256 + 256],
                                            (xtile(0, c, b, 2 * pair + t), xtile(1, c, b, 2 * pair + t)),
                                            (w_hi["v"][:, c, :], w_lo["v"][:, c, :]), c == 0, c == 1)
                    return last
                if w == "score":
                    s = name[1]
                    u, t = divmod(s, 8)
                    if t % 4 == 0:
                        pe.wait_ge(dve_s, at(DV, ("qklo", u, 2 * (t // 4) + 1), i, name))
                    prev, sh2 = ((s - 2, 0) if s >= 2 else (s + 30, -1))
                    if not (isinstance(i, int) and i + sh + sh2 < 0):
                        pe.wait_ge(act_s, AC.at(("exp", prev), i + sh + sh2 - shift["exp", prev]))
                    keys = (t + 1) * P
                    cuts = [(0, min(512, max(keys, 256)))] + ([(512, max(keys, 768))] if keys > 512 else [])
                    for a, z in cuts:
                        q = [x[u % 2][:, 0, t * P:t * P + P] for x in (qk_hi, qk_lo)]
                        k = [x[u % 2][:, 1, a:z] for x in (qk_hi, qk_lo)]
                        last = product3(nc, S[s % 2][:, a:z], q, k, True, True)
                    return last
                if w == "turn":
                    _, s, part = name
                    t, n = s % 8, tb_index[s, part]
                    needs = [done_for(("norm", s), name)] if part == 0 else []
                    of, n2 = next(k for k in tb_index.items() if k[1] == (n - 2) % len(tb_index))
                    back = -int(n < 2)
                    if not (isinstance(i, int) and i + sh + back < 0):
                        lo, later = done_for(("turnlo",) + of, name)
                        needs.append((lo, later + back))
                    if needs:
                        pe.wait_ge(dve_s, DV.latest(i, needs))
                    for k in range(4 * part, min(4 * part + 4, t + 1)):
                        last = nc.tensor.transpose(T[n % 2][:, (k % 4) * P:(k % 4) * P + P],
                                                   probs(s)[:, k * P:k * P + P], ident[:])
                    return last
                if w == "pv":
                    _, u, g = name
                    b, h = u // 2, u % 2
                    needs = [done_for(("turnlo", 8 * u + 4 * g + 3, g), name), done_for(("vlo", b, 2 * g + 1), name)]
                    pu, pg, psh = (u, 0, 0) if g else ((u - 1) % 4, 1, -int(u == 0))
                    if not (isinstance(i, int) and i + sh + psh < 0):
                        needs.append((("olo", pu, pg), sh + psh - shift[("olo", pu, pg)]))
                    pe.wait_ge(dve_s, DV.latest(i, needs))
                    for kt in range(4 * g + 4):
                        off = min(max(0, kt - 4 * g) * P, 256)
                        vv = [x[b][:, kt, h * P:h * P + P] for x in (v_hi, v_lo)]
                        pp = [x[g][:, kt, off:512] for x in (pt_hi, pt_lo)]
                        last = product3(nc, O[:, off:512], vv, pp, kt == 0, kt == 4 * g + 3)
                    return last
                _, b, g, m = name
                needs += [done_for(("olo", 2 * b + 1, g), name), done_for(("w", "o", "lo"), name)]
                pe.wait_ge(dve_s, DV.latest(i, needs))
                for h in range(2):
                    last = product3(nc, J, (w_hi["o"][:, h, m * P:m * P + P], w_lo["o"][:, h, m * P:m * P + P]),
                                    (o_hi[h][:, g, :], o_lo[h][:, g, :]), h == 0, h == 1)
                return last

            everywhere(pe, pe_s, pe_plan, PE, work)

        def turned(x, s, part):
            t = s % 8
            k0, k1 = 4 * part, min(4 * part + 4, t + 1)
            return x[t // 4][:, k0:k1, (t % 4) * P:(t % 4) * P + P], T[tb_index[s, part] % 2][:, 0:(k1 - k0) * P]\
                .rearrange("p (k n) -> p k n", n=P)

        @block.scalar
        def _(act):
            def work(name, i):
                w = name[0]
                if w == "w":
                    k = name[1]
                    act.wait_ge(s_win[k], (i + shift[name] + 1) * 16)
                    if not (isinstance(i, int) and i + shift[name] == 0):
                        last_use = {"o": ("oproj", 1, 1, 1), "v": ("v", 1, 3)}.get(k, ("qk", 3, 3))
                        act.wait_ge(pe_s, PE.at(last_use, i + shift[name] - 1 - shift[last_use]))
                    return nc.scalar.activation(w_hi[k][:], loaded(k, isinstance(i, int) and i + shift[name] == 0), ACT.Copy)
                if w == "qkhi":
                    _, u, part = name
                    act.wait_ge(pe_s, at(PE, ("qk", u, part), i, name))
                    return nc.scalar.activation(qk_hi[u % 2][:, part % 2, (part // 2) * 512:(part // 2) * 512 + 512],
                                                j_bank(("qk", u, part), i, shift[name]), ACT.Copy, scale=(SCALE, 1.0)[part % 2])
                if w == "vhi":
                    _, b, t = name
                    act.wait_ge(pe_s, at(PE, ("v", b, t), i, name))
                    return nc.scalar.activation(v_hi[b][:, 2 * t:2 * t + 2, :].rearrange("p t n -> p (t n)"),
                                                j_bank(("v", b, t), i, shift[name]), ACT.Copy)
                if w == "exp":
                    s = name[1]
                    keys = (s % 8 + 1) * P
                    act.wait_ge(dve_s, at(DV, ("max", s), i, name))
                    back = next(k for k in range(1, 32) if probs((s - k) % 32) is probs(s))
                    last, pair = ("turn", (s - back) % 32, turn_parts(s - back) - 1), shift[name] - int(back > s)
                    if not (isinstance(i, int) and i + pair < 0):
                        act.wait_ge(pe_s, PE.at(last, i + pair - shift[last]))
                    return nc.scalar.activation(probs(s)[:, 0:keys], S[s % 2][:, 0:keys], ACT.Exp,
                                                bias=nmx[:, s % 8:s % 8 + 1],
                                                accum_out=tot[:, s % 8:s % 8 + 1])
                if w == "turnhi":
                    _, s, part = name
                    act.wait_ge(pe_s, at(PE, ("turn", s, part), i, name))
                    to, of = turned(pt_hi, s, part)
                    return nc.scalar.activation(to, of, ACT.Copy)
                _, u, g = name
                act.wait_ge(pe_s, at(PE, ("pv", u, g), i, name))
                return nc.scalar.activation(o_hi[u % 2][:, g, :], O, ACT.Copy)

            everywhere(act, act_s, act_plan, AC, work)

        @block.vector
        def _(dve):
            dve.wait_ge(s_zero, 1)
            for g in range(2):
                for x in (pt_hi, pt_lo):
                    nc.vector.tensor_copy(x[g][:, 4 * g + 3, 256:384], prob0[:]).then_inc(s_pad, 1)
            dve.wait_ge(s_pad, 4)

            def work(name, i):
                w = name[0]
                if w == "w":
                    k = name[1]
                    dve.wait_ge(act_s, at(AC, ("w", k, "hi"), i, name))
                    return nc.vector.tensor_tensor(w_lo[k][:], loaded(k, isinstance(i, int) and i + shift[name] == 0),
                                                   w_hi[k][:].bitcast(F32), ALU.subtract)
                if w == "qklo":
                    _, u, part = name
                    dve.wait_ge(act_s, at(AC, ("qkhi", u, part), i, name))
                    a = (part // 2) * 512
                    to, hi = (x[u % 2][:, part % 2, a:a + 512] for x in (qk_lo, qk_hi))
                    of = j_bank(("qk", u, part), i, shift[name])
                    if part % 2 == 0:
                        return nc.vector.scalar_tensor_tensor(out=to, in0=of, scalar=SCALE, in1=hi.bitcast(F32),
                                                              op0=ALU.mult, op1=ALU.subtract)
                    return nc.vector.tensor_tensor(to, of, hi.bitcast(F32), ALU.subtract)
                if w == "vlo":
                    _, b, t = name
                    dve.wait_ge(act_s, at(AC, ("vhi", b, t), i, name))
                    to, hi = (x[b][:, 2 * t:2 * t + 2, :].rearrange("p t n -> p (t n)") for x in (v_lo, v_hi))
                    return nc.vector.tensor_tensor(to, j_bank(("v", b, t), i, shift[name]), hi.bitcast(F32), ALU.subtract)
                if w == "mask":
                    s = name[1]
                    t = s % 8
                    dve.wait_ge(pe_s, at(PE, ("score", s), i, name))
                    x = S[s % 2][:, t * P:t * P + P]
                    return nc.vector.tensor_tensor(x, x, keep["cmask"][:], ALU.add)
                if w == "max":
                    s = name[1]
                    dve.wait_ge(dve_s, at(DV, ("mask", s), i, name))
                    return nc.vector.tensor_reduce(nmx[:, s % 8:s % 8 + 1], S[s % 2][:, 0:(s % 8 + 1) * P], AX_X,
                                                   ALU.max, negate=True)
                if w == "turnlo":
                    _, s, part = name
                    dve.wait_ge(act_s, at(AC, ("turnhi", s, part), i, name))
                    to, of = turned(pt_lo, s, part)
                    hi, _ = turned(pt_hi, s, part)
                    return nc.vector.tensor_tensor(to, of, hi.bitcast(F32), ALU.subtract)
                if w == "inv":
                    s = name[1]
                    dve.wait_ge(act_s, at(AC, ("exp", s), i, name))
                    return nc.vector.reciprocal(inv[:, s % 8:s % 8 + 1], tot[:, s % 8:s % 8 + 1])
                if w == "norm":
                    s = name[1]
                    dve.wait_ge(dve_s, at(DV, ("inv", s), i, name))
                    x = probs(s)[:, 0:(s % 8 + 1) * P]
                    return nc.vector.tensor_scalar(x, x, inv[:, s % 8:s % 8 + 1], None, ALU.mult)
                if w == "olo":
                    _, u, g = name
                    dve.wait_ge(act_s, at(AC, ("ohi", u, g), i, name))
                    return nc.vector.tensor_tensor(o_lo[u % 2][:, g, :], O, o_hi[u % 2][:, g, :].bitcast(F32),
                                                   ALU.subtract)
                _, b, g, m = name
                dve.wait_ge(pe_s, at(PE, ("oproj",) + name[1:], i, name))
                y = keep["y"][:, m, :].rearrange("p (j b t) -> p j b t", j=4, b=2)[:, 2 * g:2 * g + 2, b, :]
                return nc.vector.tensor_tensor(y, y, J.rearrange("p (j t) -> p j t", j=2), ALU.add)

            everywhere(dve, dve_s, dve_plan, DV, work)


def experts(nc, ctx, sb, sem, psum, keep, dram):
    st = ExitStack()
    with st:
        def tb(name, shape, dt=F32):
            return st.enter_context(nc.sbuf_tensor(name, shape, dt))

        def esem(name):
            return sem("moe_" + name)

        N, HALF, ITER = 24, 12, PAIRS // 2
        w_in = tb("e_win", [P, 3, 768])
        w_hi = [tb(f"e_whi{k}", [P, 3, 768], F32R) for k in range(2)]
        w_lo = [tb(f"e_wlo{k}", [P, 3, 768], F32R) for k in range(2)]
        share = [tb(f"e_share{k}", [P, 3, NB * BT]) for k in range(2)]
        sg = [tb(f"e_sg{k}", [P, BT]) for k in range(2)]
        a1 = [tb(f"e_a1{k}", [P, BT]) for k in range(2)]
        af = [tb(f"e_af{k}", [P, BT]) for k in range(2)]
        ahi = [tb(f"e_ahi{k}", [P, BT], F32R) for k in range(2)]
        alo = [tb(f"e_alo{k}", [P, BT], F32R) for k in range(2)]
        E, TOPK, TT = 16, 4, 16
        ones, gw, col = tb("r_ones", [P, P]), tb("r_gw", [P, DC, E]), tb("r_col", [P, DC])
        sq, rs, x2 = ([tb(f"r_{n}{k}", s) for k in range(2)] for n, s in (("sq", [P, DC, BT]), ("rs", [P, BT]), ("x2", [P, DC, BT])))
        lg, pr, top, eq, sel = (tb(f"r_{n}", [P, TT, E]) for n in ("lg", "pr", "top", "eq", "sel"))
        rank = tb("r_rank", [P, E])
        m1, m2 = tb("r_m1", [P, TT]), tb("r_m2", [P, TT])
        wfT = tb("r_wfT", [P, 2, P])
        s_in, s_const, s_stored = esem("gate_loaded"), esem("gate_constants"), esem("route_stored")
        s_sq, s_ms, s_ln, s_r, s_x2 = (esem(n) for n in ("squares", "mean_square", "ln", "rms", "x2"))
        s_xhi, s_xlo, s_logits, s_lg = (esem(n) for n in ("x2_hi", "x2_lo", "logits", "logits_copied"))
        s_gate, s_exp, s_turn, s_turned = (esem(n) for n in ("gating", "exponentials", "turned", "turned_copied"))
        GATED = 6 + 6 * TOPK + 4
        GATING_AT = [x for n in range(HALF + 1, N) for x in (("lo", n), ("weigh", n + 1))][:2 * TOPK + 1]
        TURN_AT = 20
        G, U, DN = (lambda n: psum[:, n % 3, :]), (lambda n: psum[:, 3 + n % 3, :]), psum[:, 6:8, :]

        pe_plan, act_plan, dve_plan = [], [], []
        for n in range(N):
            pe_plan += [(("gu", (n + 2) % N), (n + 2) // N), (("down", n), 0)]
            w = {4: (1, 0, 0), 5: (1, 1, 0), 6: (1, 2, 0), 16: (0, 0, 1), 17: (0, 1, 1), 18: (0, 2, 1)}.get(n)
            act_plan += [(("silu", (n + 1) % N), (n + 1) // N), (("hi", n), 0)]
            if n % 3 == 0:
                dve_plan.append((("add", (n - 1) % N), -int(n == 0)))
            dve_plan += [(("lo", n), 0), (("weigh", (n + 1) % N), (n + 1) // N), (("act", (n + 1) % N), (n + 1) // N)]
            if w:
                act_plan.append((("w", w[0], w[1], "hi"), w[2]))
                dve_plan.append((("w", w[0], w[1], "lo"), w[2]))
        PE, AC, DV = (Steps([x for x, _ in p]) for p in (pe_plan, act_plan, dve_plan))
        shift = {**dict(pe_plan), **dict(act_plan), **dict(dve_plan)}
        pe_s, act_s, dve_s = esem("tensor_steps"), esem("scalar_steps"), esem("vector_steps")
        s_w, s_share, s_one = esem("weights_loaded"), [esem(f"share{k}_loaded") for k in range(2)], esem("share_one")

        def at(steps, name, i, of=None):
            return steps.at(name, i + (shift[of] - shift[name] if of else 0))

        def done_for(name, of):
            return name, shift[of] - shift[name]

        def pair_of(name, i):
            q = name[1] if name[0] == "w" else name[1] // HALF
            return 2 * (i + shift[name]) + 1 + q

        def run(eng, s, plan, steps, i, work, start=0, stop=None):
            known = isinstance(i, int)
            skipped = 0
            for k, (name, sh) in list(enumerate(plan))[start:stop]:
                if known and not 0 <= pair_of(name, i) < PAIRS:
                    skipped += 1
                    steps.one(name)
                    continue
                if skipped:
                    if k - skipped + (i + 1) * steps.per:
                        eng.wait_ge(s, k - skipped + (i + 1) * steps.per)
                    eng.sem_inc(s, skipped)
                    skipped = 0
                work(name, i).then_inc(s, steps.one(name))
            if skipped and i != ITER and stop is None:
                eng.wait_ge(s, k + 1 - skipped + (i + 1) * steps.per)
                eng.sem_inc(s, skipped)

        def after_first_split(plan):
            return 1 + max(k for k, (name, _) in enumerate(plan) if name[:3] == ("w", 1, 2))

        def everywhere(eng, s, plan, steps, work, start=0):
            run(eng, s, plan, steps, -1, work, start)
            with eng.Fori(0, ITER - 1) as i:
                run(eng, s, plan, steps, i, work)
            run(eng, s, plan, steps, ITER - 1, work)
            run(eng, s, plan, steps, ITER, work)

        def before(name, back, i):
            n = name[1] - back
            d = -int(n < 0)
            if isinstance(i, int) and 2 * (i + shift[name] + d) + 1 + (n % N) // HALF < 0:
                return None
            return n % N, d

        block = st.enter_context(nc.Block())

        @block.sync
        def _(sp):
            def load_weights(i, q):
                sp.wait_ge(dve_s, DV.at(("w", 1 - q, 2, "lo"), i - 1))
                sp.dma_start(w_in[:], dram["moe_w"][:, bass.ds(2 * i + 1 + q, 1)].rearrange("p a c n -> p (a c) n"))\
                    .then_inc(s_w, 16)

            def load_shares(i, q):
                sp.wait_ge(dve_s, DV.at(("weigh", 11 + 12 * q), i - 1))
                for e in range(2):
                    row = dram["route"][bass.ds(4 * i + 2 * q + e, 1), :]
                    sp.dma_start(share[q][:, e, :], row.broadcast_to([P, NB * BT])).then_inc(s_share[q], 16)
                    sp.dma_start(share[q][48 * e:48 * e + 48, 2, :], row.broadcast_to([48, NB * BT]))\
                        .then_inc(s_share[q], 16)

            sp.dma_start(col[:], dram["cols2"]).then_inc(s_in, 16)
            sp.dma_start(gw[:], dram["gate_w"]).then_inc(s_in, 16)
            sp.dma_start(w_in[:], dram["moe_w"][:, 0]).then_inc(s_w, 16)
            load_weights(0, 0)
            sp.wait_ge(s_turned, 1)
            for g in range(2):
                for t in range(8):
                    sp.dma_start(dram["route"][:, (8 * g + t) * P:(8 * g + t + 1) * P],
                                 wfT[16 * t:16 * t + 16, g, :]).then_inc(s_stored, 16)
            sp.wait_ge(s_stored, 16 * 16)
            sp.wait_ge(s_one, 2)
            with sp.Fori(0, ITER - 1) as i:
                load_shares(i, 0)
                load_weights(i, 1)
                load_shares(i, 1)
                load_weights(i + 1, 0)
            load_shares(ITER - 1, 0)
            load_weights(ITER - 1, 1)
            load_shares(ITER - 1, 1)

        @block.gpsimd
        def _(pool):
            nc.gpsimd.memset(ones[:], 1.0 / D).then_inc(s_const, 1)
            for e in range(E):
                nc.gpsimd.memset(rank[:, e:e + 1], float(E - e)).then_inc(s_const, 1)
            for q in (1, 0):
                nc.gpsimd.memset(share[q][:], 1.0).then_inc(s_one, 1)

        @block.tensor
        def _(pe):
            def mean_square(b):
                pe.wait_ge(s_sq, b + 1)
                if b >= 2:
                    pe.wait_ge(s_ln, b - 1)
                for c in range(DC):
                    last = nc.tensor.matmul(psum[:, 6 + b % 2, :], ones[:], sq[b % 2][:, c, :], start=c == 0, stop=c == 1)
                last.then_inc(s_ms, 1)

            def logits(b):
                pe.wait_ge(s_x2, 2 * b + 2)
                for t in range(4):
                    for c in range(DC):
                        last = nc.tensor.matmul(psum[:, 5, (4 * b + t) * E:(4 * b + t + 1) * E],
                                                x2[b % 2][:, c, t * P:t * P + P], gw[:, c, :], start=c == 0, stop=c == 1)
                last.then_inc(s_logits, 1)

            def turn_weights(out):
                pe.wait_ge(s_gate, GATED)
                for g in range(2):
                    last = nc.tensor.transpose(out[:, g * P:g * P + P],
                                               top[:, 8 * g:8 * g + 8, :].rearrange("p t e -> p (t e)"), keep["ident"][:])
                last.then_inc(s_turn, 1)

            pe.wait_ge(s_const, 1)
            pe.wait_ge(s_in, 32)
            mean_square(0)
            mean_square(1)
            for b in range(2):
                logits(b)
                mean_square(b + 2)
            def work(name, i):
                n = name[1]
                q, t, j = n // HALF, (n % HALF) // 3, n % 3
                needs = []
                if name[0] == "gu":
                    if n % HALF == 0:
                        needs.append(done_for(("w", q, 1, "lo"), name))
                    p = before(name, 3, i)
                    if p:
                        done, later = done_for(("act", p[0]), name)
                        needs.append((done, later + p[1]))
                    if needs:
                        pe.wait_ge(dve_s, DV.latest(i, needs))
                    if isinstance(i, int) and i + shift[name] == -1 and j == 0:
                        pe.wait_ge(s_xlo, t + 1)
                    if isinstance(i, int) and i + shift[name] == -1 and n in (HALF + 1, HALF + 2):
                        logits(n - HALF + 1)
                    if isinstance(i, int) and i + shift[name] == -1 and n == HALF + 2:
                        pe.wait_ge(s_lg, 1)
                    if isinstance(i, int) and i == -1 and n == TURN_AT:
                        turn_weights(G(n))
                        pe.wait_ge(s_turned, 1)
                    for g, out in enumerate((G(n), U(n))):
                        for c in range(DC):
                            o = g * 384 + j * P
                            last = product3(nc, out, (w_hi[q][:, c, o:o + P], w_lo[q][:, c, o:o + P]),
                                            (keep["xx_hi"][:, c, t * BT:t * BT + BT], keep["xx_lo"][:, c, t * BT:t * BT + BT]),
                                            c == 0, c == 1)
                    return last
                needs = [done_for(("lo", n), name)]
                if n % HALF == 0:
                    needs.append(done_for(("w", q, 2, "lo"), name))
                if j == 0:
                    p = before(name, 1, i)
                    if p:
                        add, later = done_for(("add", p[0]), name)
                        needs.append((add, later + p[1]))
                pe.wait_ge(dve_s, DV.latest(i, needs))
                for m in range(2):
                    o = j * D + m * P
                    last = product3(nc, DN[:, m, :], (w_hi[q][:, 2, o:o + P], w_lo[q][:, 2, o:o + P]),
                                    (ahi[n % 2][:], alo[n % 2][:]), j == 0, j == 2)
                return last

            everywhere(pe, pe_s, pe_plan, PE, work)

        @block.scalar
        def _(act):
            def squares(b):
                if b >= 2:
                    act.wait_ge(s_ms, b - 1)
                nc.scalar.activation(sq[b % 2][:], keep["y"][:, :, b * BT:b * BT + BT], ACT.Square).then_inc(s_sq, 1)

            def work(name, i):
                if isinstance(i, int) and i == -1 and name == ("silu", TURN_AT):
                    act.wait_ge(s_turn, 1)
                    nc.scalar.activation(wfT[:].rearrange("p g n -> p (g n)"), G(TURN_AT)[:, 0:2 * P], ACT.Copy)\
                        .then_inc(s_turned, 1)
                if name[0] == "w":
                    _, q, part, _ = name
                    if part == 0:
                        act.wait_ge(s_w, (pair_of(name, i) + 1) * 16)
                        if not (isinstance(i, int) and pair_of(name, i) < 2):
                            act.wait_ge(pe_s, PE.at(("down", 12 * q + 11), i + shift[name] - 1))
                    return nc.scalar.activation(w_hi[q][:, part, :], w_in[:, part, :], ACT.Copy)
                n = name[1]
                if name[0] == "silu":
                    act.wait_ge(pe_s, at(PE, ("gu", n), i, name))
                    return nc.scalar.activation(sg[n % 2][:], G(n), ACT.Silu)
                act.wait_ge(dve_s, at(DV, ("act", n), i, name))
                p = before(name, 2, i)
                if p:
                    act.wait_ge(pe_s, at(PE, ("down", p[0]), i + p[1], name))
                return nc.scalar.activation(ahi[n % 2][:], af[n % 2][:], ACT.Copy)

            load_ln_exp(nc, act)
            squares(0)
            squares(1)
            for b in range(NB):
                if b == 1:
                    run(act, act_s, act_plan, AC, -1, work, stop=after_first_split(act_plan))
                act.wait_ge(s_ms, b + 1)
                if b >= 2:
                    act.wait_ge(s_x2, 2 * b - 2)
                nc.scalar.activation(rs[b % 2][:], psum[:, 6 + b % 2, :], ACT.Ln, bias=keep["eps"][:, 1:2]).then_inc(s_ln, 1)
                act.wait_ge(s_ln, b + 1)
                nc.scalar.activation(rs[b % 2][:], rs[b % 2][:], ACT.Exp, scale=-0.5).then_inc(s_r, 1)
                if b + 2 < NB:
                    squares(b + 2)
                act.wait_ge(s_x2, 2 * b + 2)
                nc.scalar.activation(keep["xx_hi"][:, :, b * BT:b * BT + BT], x2[b % 2][:], ACT.Copy).then_inc(s_xhi, 1)
            act.wait_ge(s_logits, NB)
            nc.scalar.activation(lg[:].rearrange("p t e -> p (t e)"), psum[:, 5, 0:TT * E], ACT.Copy).then_inc(s_lg, 1)
            act.wait_ge(s_gate, 2)
            nc.scalar.activation(pr[:], lg[:], ACT.Exp).then_inc(s_exp, 1)

            everywhere(act, act_s, act_plan, AC, work, after_first_split(act_plan))

        @block.vector
        def _(dve):
            n_gate = [0]

            def link(ins):
                n_gate[0] += 1
                ins.then_inc(s_gate, 1)
                dve.wait_ge(s_gate, n_gate[0])

            def wide(ap):
                return ap.unsqueeze(2).broadcast_to([P, TT, E])

            def softmax():
                link(nc.vector.reduce_sum(m1[:], pr[:], AX_X))
                link(nc.vector.reciprocal(m2[:], m1[:]))
                link(nc.vector.tensor_tensor(pr[:], pr[:], wide(m2[:]), ALU.mult))
                link(nc.vector.tensor_copy(top[:], pr[:]))

            def largest():
                link(nc.vector.reduce_max(m1[:], top[:], AX_X))
                link(nc.vector.tensor_tensor(eq[:], top[:], wide(m1[:]), ALU.is_equal))
                link(nc.vector.tensor_tensor(eq[:], eq[:], rank[:].unsqueeze(1).broadcast_to([P, TT, E]), ALU.mult))

            def lower_it():
                link(nc.vector.reduce_max(m2[:], eq[:], AX_X))
                link(nc.vector.tensor_tensor(sel[:], eq[:], wide(m2[:]), ALU.is_equal))
                link(nc.vector.scalar_tensor_tensor(out=top[:], in0=sel[:], scalar=-4.0, in1=top[:], op0=ALU.mult,
                                                    op1=ALU.add))

            def chosen():
                link(nc.vector.scalar_tensor_tensor(out=top[:], in0=top[:], scalar=-1.0, in1=pr[:], op0=ALU.is_lt,
                                                    op1=ALU.mult))
                link(nc.vector.reduce_sum(m1[:], top[:], AX_X))
                link(nc.vector.reciprocal(m2[:], m1[:]))
                link(nc.vector.tensor_tensor(top[:], top[:], wide(m2[:]), ALU.mult))
                assert n_gate[0] == GATED

            def work(name, i):
                if isinstance(i, int) and i == -1 and name in GATING_AT:
                    k = GATING_AT.index(name)
                    if k < 2 * TOPK:
                        (largest, lower_it)[k % 2]()
                    else:
                        chosen()
                if name[0] == "w":
                    _, q, part, _ = name
                    dve.wait_ge(act_s, at(AC, ("w", q, part, "hi"), i, name))
                    return nc.vector.tensor_tensor(w_lo[q][:, part, :], w_in[:, part, :],
                                                   w_hi[q][:, part, :].bitcast(F32), ALU.subtract)
                n = name[1]
                q, t, j = n // HALF, (n % HALF) // 3, n % 3
                if name[0] == "weigh":
                    act_done = at(PE, ("gu", n), i, name)
                    dve.wait_ge(pe_s, act_done)
                    if n % HALF == 0 and not (isinstance(i, int) and pair_of(name, i) == 0):
                        dve.wait_ge(s_share[q], (i + shift[name] + 1) * 64)
                    return nc.vector.tensor_tensor(a1[n % 2][:], U(n), share[q][:, j, t * BT:t * BT + BT], ALU.mult)
                if name[0] == "act":
                    dve.wait_ge(dve_s, at(DV, ("weigh", n), i, name))
                    dve.wait_ge(act_s, at(AC, ("silu", n), i, name))
                    return nc.vector.tensor_tensor(af[n % 2][:], a1[n % 2][:], sg[n % 2][:], ALU.mult)
                if name[0] == "lo":
                    dve.wait_ge(act_s, at(AC, ("hi", n), i, name))
                    return nc.vector.tensor_tensor(alo[n % 2][:], af[n % 2][:], ahi[n % 2][:].bitcast(F32), ALU.subtract)
                dve.wait_ge(pe_s, at(PE, ("down", n), i, name))
                y = keep["y"][:, :, t * BT:t * BT + BT]
                return nc.vector.tensor_tensor(y, y, DN, ALU.add)

            dve.wait_ge(s_in, 32)
            for b in range(NB):
                if b == 1:
                    run(dve, dve_s, dve_plan, DV, -1, work, stop=after_first_split(dve_plan))
                dve.wait_ge(s_r, b + 1)
                if b >= 2:
                    dve.wait_ge(s_xlo, b - 1)
                    dve.wait_ge(s_logits, b - 1)
                for c in range(DC):
                    nc.vector.scalar_tensor_tensor(out=x2[b % 2][:, c, :], in0=keep["y"][:, c, b * BT:b * BT + BT],
                                                   scalar=col[:, c:c + 1], in1=rs[b % 2][:], op0=ALU.mult, op1=ALU.mult)\
                        .then_inc(s_x2, 1)
                dve.wait_ge(s_xhi, b + 1)
                nc.vector.tensor_tensor(keep["xx_lo"][:, :, b * BT:b * BT + BT], x2[b % 2][:],
                                        keep["xx_hi"][:, :, b * BT:b * BT + BT].bitcast(F32), ALU.subtract).then_inc(s_xlo, 1)
            dve.wait_ge(s_const, 1 + E)
            dve.wait_ge(s_lg, 1)
            link(nc.vector.reduce_max(m1[:], lg[:], AX_X))
            link(nc.vector.tensor_tensor(lg[:], lg[:], wide(m1[:]), ALU.subtract))
            dve.wait_ge(s_exp, 1)
            softmax()
            dve.wait_ge(s_one, 1)

            everywhere(dve, dve_s, dve_plan, DV, work, after_first_split(dve_plan))


def last_norm(nc, ctx, sb, sem, psum, keep, dram):
    st = ExitStack()
    with st:
        def tb(name, shape, dt=F32):
            return st.enter_context(nc.sbuf_tensor(name, shape, dt))

        def fsem(name):
            return sem("last_" + name)

        ones, rs = tb("f_ones", [P, P]), [tb(f"f_rs{k}", [P, BT]) for k in range(2)]
        x1 = tb("f_x1", [P, DC, NB * BT])
        xc, sq, out = ([tb(f"f_{n}{k}", [P, DC, BT]) for k in range(2)] for n in ("xc", "sq", "out"))
        s_x1 = [fsem(f"x1_loaded{b}") for b in range(NB)]
        s_one, s_mean, s_var, s_sq = fsem("ones"), fsem("mean"), fsem("variance"), fsem("squares")
        s_ln, s_r, s_xc, s_xn, s_sum = (fsem(n) for n in ("ln", "rstd", "centered", "normed", "sum"))
        s_out = [fsem(f"stored{k}") for k in range(2)]
        block = st.enter_context(nc.Block())

        def bc2(ap):
            return ap.unsqueeze(1).broadcast_to([P, DC, BT])

        @block.sync
        def _(sp):
            for b in range(NB):
                sp.dma_start(x1[:, :, b * BT:b * BT + BT], dram["x1"][:, :, b * BT:b * BT + BT]).then_inc(s_x1[b], 16)
            for b in range(NB):
                sp.wait_ge(s_sum, b + 1)
                sp.dma_start(dram["outT"][:, :, b * BT:b * BT + BT], out[b % 2][:]).then_inc(s_out[b % 2], 16)
            for k in range(2):
                sp.wait_ge(s_out[k], 16 * NB // 2)

        @block.gpsimd
        def _(pool):
            nc.gpsimd.memset(ones[:], 1.0 / D).then_inc(s_one, 1)
            for b in range(NB):
                pool.wait_ge(s_xn, b + 1)
                pool.wait_ge(s_x1[b], 16)
                nc.gpsimd.tensor_tensor(out[b % 2][:], out[b % 2][:], x1[:, :, b * BT:b * BT + BT], ALU.add)\
                    .then_inc(s_sum, 1)

        @block.tensor
        def _(pe):
            pe.wait_ge(s_one, 1)

            def mean(b):
                if b >= 2:
                    pe.wait_ge(s_xc, b - 1)
                for c in range(DC):
                    last = nc.tensor.matmul(psum[:, b % 2, :], ones[:], keep["y"][:, c, b * BT:b * BT + BT],
                                            start=c == 0, stop=c == 1)
                last.then_inc(s_mean, 1)

            mean(0)
            for b in range(NB):
                if b + 1 < NB:
                    mean(b + 1)
                pe.wait_ge(s_sq, b + 1)
                if b >= 2:
                    pe.wait_ge(s_ln, b - 1)
                for c in range(DC):
                    last = nc.tensor.matmul(psum[:, 2 + b % 2, :], ones[:], sq[b % 2][:, c, :], start=c == 0, stop=c == 1)
                last.then_inc(s_var, 1)

        @block.scalar
        def _(act):
            load_ln_exp(nc, act)
            for b in range(NB):
                act.wait_ge(s_xc, b + 1)
                nc.scalar.activation(sq[b % 2][:], xc[b % 2][:], ACT.Square).then_inc(s_sq, 1)
                act.wait_ge(s_var, b + 1)
                if b >= 2:
                    act.wait_ge(s_xn, b - 1)
                nc.scalar.activation(rs[b % 2][:], psum[:, 2 + b % 2, :], ACT.Ln, bias=keep["eps"][:, 0:1]).then_inc(s_ln, 1)
                act.wait_ge(s_ln, b + 1)
                nc.scalar.activation(rs[b % 2][:], rs[b % 2][:], ACT.Exp, scale=-0.5).then_inc(s_r, 1)

        @block.vector
        def _(dve):
            def center(b):
                dve.wait_ge(s_mean, b + 1)
                if b >= 2:
                    dve.wait_ge(s_sq, b - 1)
                    dve.wait_ge(s_xn, b - 1)
                nc.vector.tensor_tensor(xc[b % 2][:], keep["y"][:, :, b * BT:b * BT + BT], bc2(psum[:, b % 2, :]),
                                        ALU.subtract).then_inc(s_xc, 1)

            center(0)
            for b in range(NB):
                if b + 1 < NB:
                    center(b + 1)
                dve.wait_ge(s_r, b + 1)
                if b >= 2:
                    dve.wait_ge(s_out[b % 2], 16 * (b // 2))
                nc.vector.tensor_tensor(out[b % 2][:], xc[b % 2][:], bc2(rs[b % 2][:]), ALU.mult).then_inc(s_xn, 1)


def build(nc, dram):
    ctx = ExitStack()
    with ctx:
        def sb(name, shape, dt=F32):
            return ctx.enter_context(nc.sbuf_tensor(name, shape, dt))

        def sem(name):
            return ctx.enter_context(nc.semaphore(name))

        psum = ctx.enter_context(nc.psum_tensor("psum", [P, 8, 512], F32))
        keep = {"y": sb("y", [P, DC, NB * BT]), "xx_hi": sb("xx_hi", [P, DC, NB * BT], F32R),
                "xx_lo": sb("xx_lo", [P, DC, NB * BT], F32R), "ident": sb("ident", [P, P]),
                "cmask": sb("cmask", [P, P]), "eps": sb("eps", [P, 3])}
        gla_layer(nc, ctx, sb, sem, psum, keep, dram)
        attention_layer(nc, ctx, sb, sem, psum, keep, dram)
        experts(nc, ctx, sb, sem, psum, keep, dram)
        last_norm(nc, ctx, sb, sem, psum, keep, dram)


def kernel(**inputs):
    import numpy as np
    import concourse.bacc as bacc
    from concourse.bass_utils import run_bass_kernel_spmd

    a = {k: np.asarray(v) for k, v in inputs.items()}
    f = np.float32

    def rows(w):
        return w.reshape(DC, P, -1).transpose(1, 0, 2)

    def turned_tokens(x):
        return x.reshape(2, NB, 256, DC, P).transpose(4, 3, 1, 0, 2).reshape(P, DC, NB * BT)

    A, B = "L0_attn_", "L0_ffn_"
    arrays = {"xT": turned_tokens(a[A + "x"])}
    for n in ("wq", "wk", "wv", "wg", "wo", "gk_w1", "gk_w2", "w_gate", "w_up", "w_down"):
        arrays[n] = a[A + n]
    col = lambda w: w.reshape(DC, P).T
    arrays["cols"] = np.concatenate([col(a[A + "norm1_w"]), col(a[A + "ffn_norm_w"]), col(a[B + "ln1_w"]),
                                     a[A + "gk_b"][:, None], np.tile(a[A + "gnorm_w"], 4)[:, None]], axis=1)
    arrays["cols2"] = col(a[B + "ln2_w"])

    def heads(w):
        return w.reshape(8, 2, P, DC, P).transpose(4, 0, 3, 1, 2).reshape(P, 8, DC, 2 * P)

    kv = a[B + "kv_w"]
    arrays["aw_q"] = heads(a[B + "q_w"].reshape(HEADS, QHD, D)[:, :P])
    arrays["aw_k"] = heads(kv[:HEADS * P].reshape(HEADS, P, D))
    arrays["aw_v"] = heads(kv[HEADS * P:2 * HEADS * P].reshape(HEADS, P, D))
    arrays["aw_o"] = a[B + "o_w"].reshape(D, 8, 2, P).transpose(3, 1, 2, 0)
    arrays["gate_w"] = rows(a[B + "gate_w"].T)

    w = np.zeros((PAIRS, 3, P, 768), f)
    w1, w2 = a[B + "w1"], a[B + "w2"]
    I, R = w2.shape[2], w2.shape[2] - P
    sgu, sdn = a[B + "sh_gu_w"], a[B + "sh_down_w"]
    w2v = w[:, 2].reshape(PAIRS, P, 3, D)
    for g in range(2):
        w[0, 0:2, :, g * 384:g * 384 + 2 * I] = sgu[g * 2 * I:(g + 1) * 2 * I].T.reshape(DC, P, 2 * I)
        for e in range(2):
            one = w1[e::2, g * I:(g + 1) * I].transpose(0, 2, 1).reshape(8, DC, P, I)
            w[1:, 0:2, :, g * 384 + e * P:g * 384 + (e + 1) * P] = one[..., :P]
            w[1:, 0:2, :, g * 384 + 2 * P + e * R:g * 384 + 2 * P + (e + 1) * R] = one[..., P:]
    for e in range(2):
        w2v[0, :, e, :] = sdn[:, e * P:(e + 1) * P].T
        w2v[1:, :, e, :] = w2[e::2, :, :P].transpose(0, 2, 1)
        w2v[1:, e * R:(e + 1) * R, 2, :] = w2[e::2, :, P:].transpose(0, 2, 1)
    w2v[0, :2 * R, 2, :] = sdn[:, 2 * P:].T
    arrays["moe_w"] = w.transpose(2, 0, 1, 3)

    nc = bacc.Bacc("TRN2", target_bir_lowering=False, num_devices=1)
    dram, args = {}, {}
    for n, x in arrays.items():
        x = np.ascontiguousarray(x)
        args["in_" + n] = x
        dram[n] = nc.dram_tensor("in_" + n, x.shape, mybir.dt.from_np(x.dtype), kind="ExternalInput").ap()
    dram["outT"] = nc.dram_tensor("outT", (P, DC, NB * BT), F32, kind="ExternalOutput").ap()
    dram["x1"] = nc.dram_tensor("x1", (P, DC, NB * BT), F32, kind="Internal").ap()
    dram["route"] = nc.dram_tensor("route", (16, NB * BT), F32, kind="Internal").ap()
    build(nc, dram)
    r = run_bass_kernel_spmd(nc, [args], core_ids=[0])
    o = r.results[0]["outT"].reshape(P, DC, NB, 2, 256)
    return o.transpose(3, 2, 4, 1, 0).reshape(2, NB * 256, D)
```
